# Optimizing a Trainium2 kernel written in Bass

```python
import numpy as np
import jax
import jax.numpy as jnp

def _softmax(x, axis=-1):
    return jax.nn.softmax(x, axis=axis)

def _gelu(x):
    return jax.nn.gelu(x, approximate=True)

def _silu(x):
    return jax.nn.silu(x)

def _sigmoid(x):
    return jax.nn.sigmoid(x)

def _layernorm(x, axis=-1, eps=1e-05):
    m = jnp.mean(x, axis=axis, keepdims=True)
    v = jnp.var(x, axis=axis, keepdims=True)
    return (x - m) / jnp.sqrt(v + eps)

def _scatter_add(tgt, idx, src, axis=0):
    return tgt.at[idx].add(src)

def _segment_sum(src, seg, n):
    return jax.ops.segment_sum(src, seg, n)
kernel_name = 'mk_gnn_preln_d2_gnn_r8_8d78fa'

def setup_inputs(seed: int=0):
    np.random.seed(seed)
    _w = jnp.asarray

    def _rec_inputs():
        import jax
        import jax.numpy as jnp
        _gk = jax.random.key(seed)
        x = -0.0003713 + 1 * jax.random.normal(jax.random.fold_in(_gk, 1), (12500, 128), jnp.float32)
        src = jax.random.randint(jax.random.fold_in(_gk, 2), (200000,), 0, 12500, jnp.int32)
        dst = jnp.minimum((12500 * jax.random.uniform(jax.random.fold_in(_gk, 3), (200000,)) ** 2.0).astype(jnp.int32), 99999)
        _o = jnp.argsort(dst, stable=True)
        src = src[_o]
        dst = dst[_o]
        edge_attr_128 = 5.93493e-05 + 1.00006 * jax.random.normal(jax.random.fold_in(_gk, 12), (200000, 128), jnp.float32)
        edge_attr_64 = -5.16925e-05 + 1.00005 * jax.random.normal(jax.random.fold_in(_gk, 13), (200000, 64), jnp.float32)
        return (x, src, dst, edge_attr_128, edge_attr_64)
    x, src, dst, edge_attr_128, edge_attr_64 = _rec_inputs()

    def _L0_gnn_setup():
        import jax, jax.numpy as jnp
        import numpy as np
        N_NODES = 12500
        N_EDGES = 200000
        IN_DIM = 128
        OUT_DIM = 128
        EDGE_DIM = 64
        key = jax.random.key(seed)
        ks = jax.random.split(key, 8)
        x = jax.random.normal(ks[0], (N_NODES, IN_DIM), dtype=jnp.float32)
        edge_index = jax.random.randint(ks[1], (2, N_EDGES), 0, N_NODES, dtype=jnp.int64)
        edge_attr = jax.random.normal(ks[2], (N_EDGES, EDGE_DIM), dtype=jnp.float32)
        s_self = 1.0 / np.sqrt(IN_DIM)
        s_neigh = 1.0 / np.sqrt(OUT_DIM)
        s_edge = 1.0 / np.sqrt(EDGE_DIM)
        s_fin = 1.0 / np.sqrt(2 * OUT_DIM)
        W_self = jax.random.uniform(ks[3], (OUT_DIM, IN_DIM), jnp.float32, -s_self, s_self)
        W_neigh = jax.random.uniform(ks[4], (OUT_DIM, OUT_DIM), jnp.float32, -s_neigh, s_neigh)
        W_edge = jax.random.uniform(ks[5], (OUT_DIM, EDGE_DIM), jnp.float32, -s_edge, s_edge)
        W_final = jax.random.uniform(ks[6], (OUT_DIM, 2 * OUT_DIM), jnp.float32, -s_fin, s_fin)
        b_final = jax.random.uniform(ks[7], (OUT_DIM,), jnp.float32, -s_fin, s_fin)
        return {'x': x, 'edge_index': edge_index, 'edge_attr': edge_attr, 'W_self': W_self, 'W_neigh': W_neigh, 'W_edge': W_edge, 'W_final': W_final, 'b_final': b_final}
    _L0_gnn_all = _L0_gnn_setup()
    _L0_gnn_in = {k: v for k, v in _L0_gnn_all.items() if k in ('W_self', 'W_neigh', 'W_edge', 'W_final', 'b_final')}
    del _L0_gnn_all

    def _L1_gnn_setup():
        import jax, jax.numpy as jnp
        import numpy as np
        N_NODES = 6250
        N_EDGES = 75000
        HIDDEN = 128
        N_GRAPHS = 32
        key = jax.random.key(seed)
        ks = jax.random.split(key, 8)
        x = jax.random.normal(ks[0], (N_NODES, HIDDEN), dtype=jnp.float32)
        edge_index = jax.random.randint(ks[1], (2, N_EDGES), 0, N_NODES, dtype=jnp.int64)
        edge_attr = jax.random.normal(ks[2], (N_EDGES, HIDDEN), dtype=jnp.float32)
        u = jax.random.normal(ks[3], (N_GRAPHS, HIDDEN), dtype=jnp.float32)
        batch = jax.random.randint(ks[4], (N_NODES,), 0, N_GRAPHS, dtype=jnp.int64)
        s1 = 1.0 / np.sqrt(2 * HIDDEN)
        s2 = 1.0 / np.sqrt(HIDDEN)
        W1 = jax.random.uniform(ks[5], (2 * HIDDEN, HIDDEN), jnp.float32, -s1, s1)
        b1 = jnp.zeros((HIDDEN,), jnp.float32)
        W2 = jax.random.uniform(ks[6], (HIDDEN, HIDDEN), jnp.float32, -s2, s2)
        b2 = jnp.zeros((HIDDEN,), jnp.float32)
        return {'x': x, 'edge_index': edge_index, 'edge_attr': edge_attr, 'u': u, 'batch': batch, 'W1': W1, 'b1': b1, 'W2': W2, 'b2': b2}
    _L1_gnn_all = _L1_gnn_setup()
    _L1_gnn_in = {k: v for k, v in _L1_gnn_all.items() if k in ('u', 'W1', 'b1', 'W2', 'b2')}
    del _L1_gnn_all
    return {'x': x, 'src': src, 'dst': dst, 'edge_attr_128': edge_attr_128, 'edge_attr_64': edge_attr_64, 'L0_gnn_W_self': _L0_gnn_in['W_self'], 'L0_gnn_W_neigh': _L0_gnn_in['W_neigh'], 'L0_gnn_W_edge': _L0_gnn_in['W_edge'], 'L0_gnn_W_final': _L0_gnn_in['W_final'], 'L0_gnn_b_final': _L0_gnn_in['b_final'], 'L1_gnn_u': _L1_gnn_in['u'], 'L1_gnn_W1': _L1_gnn_in['W1'], 'L1_gnn_b1': _L1_gnn_in['b1'], 'L1_gnn_W2': _L1_gnn_in['W2'], 'L1_gnn_b2': _L1_gnn_in['b2']}

def reference(x, src, dst, edge_attr_128, edge_attr_64, L0_gnn_W_self, L0_gnn_W_neigh, L0_gnn_W_edge, L0_gnn_W_final, L0_gnn_b_final, L1_gnn_u, L1_gnn_W1, L1_gnn_b1, L1_gnn_W2, L1_gnn_b2):
    import jax
    import jax.numpy as jnp

    def _L0_gnn_ref(x, edge_index, edge_attr, W_self, W_neigh, W_edge, W_final, b_final):
        import jax, jax.numpy as jnp
        import numpy as np
        N_NODES = 12500
        N_EDGES = 200000
        IN_DIM = 128
        OUT_DIM = 128
        EDGE_DIM = 64
        dst = edge_index[1]
        num_nodes = x.shape[0]
        out_self = x @ W_self.T
        edge_projected = edge_attr @ W_edge.T
        aggregated = jax.ops.segment_sum(edge_projected, dst, num_segments=num_nodes)
        degree = jax.ops.segment_sum(jnp.ones((dst.shape[0],), x.dtype), dst, num_segments=num_nodes)
        degree = jnp.clip(degree, 1.0)
        aggregated = aggregated / degree[:, None]
        out_neigh = aggregated @ W_neigh.T
        h_combined = jnp.concatenate([out_self, out_neigh], axis=1)
        return h_combined @ W_final.T + b_final

    def _L1_gnn_ref(x, edge_index, edge_attr, u, batch, W1, b1, W2, b2):
        import jax, jax.numpy as jnp
        import numpy as np
        N_NODES = 6250
        N_EDGES = 75000
        HIDDEN = 128
        N_GRAPHS = 32
        col = edge_index[1]
        agg = jax.ops.segment_sum(edge_attr, col, num_segments=x.shape[0])
        combined = jnp.concatenate([x, agg], axis=1)
        h = jax.nn.relu(combined @ W1 + b1)
        return h @ W2 + b2
    edge_index = jnp.stack([src, dst])
    batch0 = jnp.zeros((12500,), jnp.int32)
    h = jnp.maximum(_layernorm(x, axis=-1), 0.0)
    x = x + _L0_gnn_ref(h, edge_index, edge_attr_64, L0_gnn_W_self, L0_gnn_W_neigh, L0_gnn_W_edge, L0_gnn_W_final, L0_gnn_b_final)
    h = jnp.maximum(_layernorm(x, axis=-1), 0.0)
    x = x + _L1_gnn_ref(h, edge_index, edge_attr_128, L1_gnn_u, batch0, L1_gnn_W1, L1_gnn_b1, L1_gnn_W2, L1_gnn_b2)
    return x

_drawn_inputs = setup_inputs


def setup_inputs(seed=0):
    import zlib

    import numpy as np

    out = dict(_drawn_inputs(seed))
    spreads = {'L1_gnn_b1': (0.0, 0.1), 'L1_gnn_b2': (0.0, 0.1)}
    factors = {}
    for name, (base, spread) in spreads.items():
        noise = np.random.default_rng([zlib.crc32(name.encode()), seed]).standard_normal(out[name].shape)
        drawn = base * np.exp(spread * noise) if base else spread * noise
        out[name] = jnp.asarray(drawn.astype(out[name].dtype))
    for name, factor in factors.items():
        out[name] = (out[name] * factor).astype(out[name].dtype)
    return out
```

```python
from contextlib import ExitStack

import concourse.bass as bass
from concourse import mybir

F32 = mybir.dt.float32
BF16 = mybir.dt.bfloat16
I32 = mybir.dt.int32
ALU = mybir.AluOpType
ACT = mybir.ActivationFunctionType
AX = mybir.AxisListType
DVE_ONLY = [mybir.EngineType.DVE]

P = 128
EPS = 1e-5


def build_gnn(nc, x, dst, edge_attr_128, edge_attr_64, W_self, W_neigh, W_edge, W_final, b_final,
              W1, b1, W2, b2, out):
    N, D = x.shape
    E = dst.shape[0]
    D64 = edge_attr_64.shape[1]

    WIN = 32
    TPQ = P // WIN
    QE = TPQ * P
    PLW = 96
    TILES = -(-E // P)
    QUADS = -(-E // QE)
    QPC = 2
    SLOTS = 4
    QPI = QPC * SLOTS
    TURNS = E // (QE * QPI)
    TPC = QPC * TPQ
    VQ = (TURNS + 1) * QPI
    VC = VQ // QPC
    LQ = QUADS - TURNS * QPI
    TAIL_E = E - (QUADS - 1) * QE
    assert VQ - QUADS == 1 and LQ % QPC == 1
    TR = -(-TILES // P)
    TABLE = VQ * TPQ

    NT = -(-N // P)
    GN = 4
    GROUPS = -(-NT // GN)
    NPAD = GROUPS * GN * P
    LAST_N = N - (NT - 1) * P
    PAIRS = TURNS + 1
    assert PAIRS * 2 == NT
    GEN_PASSES = -(-N // WIN)
    assert GEN_PASSES * WIN + PLW <= NPAD

    with ExitStack() as ctx:
        def sb(name, shape, dt=F32):
            return ctx.enter_context(nc.sbuf_tensor(name, shape, dt))

        def psum(name, shape):
            return ctx.enter_context(nc.psum_tensor(name, shape, F32))

        def sem(name):
            return ctx.enter_context(nc.semaphore(name))

        agg = sb("agg", [P, 2, NPAD])
        x0 = sb("x0", [P, GROUPS * GN, D])
        ring128 = sb("ring128", [P, SLOTS, TPC, D])
        ring64 = sb("ring64", [P, SLOTS, TPC, D64])
        rel = sb("rel", [P, TABLE])
        rowpos = sb("rowpos", [P, VQ])
        base_f = sb("base_f", [1, VQ])
        base_i = sb("base_i", [1, VQ], I32)
        onehot = sb("onehot", [P, 2, TPC, WIN])
        place = sb("place", [P, 2, QPC, PLW])
        part = sb("part", [P, 2, 200])
        xn = sb("xn", [P, 2, D])
        xb = sb("xb", [P, 2, D])
        hn = sb("hn", [P, 2, D])
        hT = sb("hT", [P, 2, P])
        w_a = sb("w_a", [P, D])
        w_c = sb("w_c", [D64 + 1, D + 1])
        w1a = sb("w1a", [P, D])
        w1b = sb("w1b", [P, D])
        w2 = sb("w2", [P, D])
        b0_bc = sb("b0_bc", [P, D])
        b2_bc = sb("b2_bc", [P, D])
        b1_col = sb("b1_col", [P, 1])
        ident = sb("ident", [P, P])
        ones_f = sb("ones_f", [P, P])
        ones_h = sb("ones_h", [P, 1], BF16)
        iota_win = sb("iota_win", [P, PLW])
        row_in_win = sb("row_in_win", [P, 1])
        eps = sb("eps", [P, 1])
        bn = sb("bn", [P, GN, 6])
        mv = sb("mv", [P, GN, 2])
        std = sb("std", [P, GN])
        rstd = sb("rstd", [P, GN])
        nmr = sb("nmr", [P, GN])
        deg = sb("deg", [P, GN])
        rdeg = sb("rdeg", [P, GN])
        chk = sb("chk", [P, 16])
        viol = sb("viol", [P, 16])
        nviol = sb("nviol", [P, 1])
        gen = sb("gen", [P, 1])
        fast = sb("fast", [P, 1])
        step = sb("step", [P, 1])
        npass = sb("npass", [1, 1], I32)

        flat = x0[:, :, :].rearrange("p t f -> p (t f)")
        TW = TR * P
        dst_i = flat[:, 0:TW].bitcast(I32).rearrange("p (c e) -> p c e", c=TR)
        dst_f = flat[:, TW:2 * TW].rearrange("p (c e) -> p c e", c=TR)
        dst_t = flat[:, 2 * TW:3 * TW]
        first = flat[:, 3 * TW:4 * TW]
        first_off = flat[:, 4 * TW:5 * TW]
        place_off = flat[:, 5 * TW:6 * TW]
        wbase = 6 * TW
        ws_raw = flat[:, wbase:wbase + D]
        wn_raw = flat[:, wbase + D:wbase + 2 * D]
        wf_raw = flat[:, wbase + 2 * D:wbase + 4 * D]
        wfT = flat[:, wbase + 4 * D:wbase + 6 * D].rearrange("p (h o) -> p h o", h=2)
        t1 = flat[:, wbase + 6 * D:wbase + 7 * D]
        we_raw = flat[:, wbase + 7 * D:wbase + 7 * D + D64]
        assert wbase + 8 * D <= NPAD

        r128 = ring128[:, :, :, :].rearrange("p s t f -> p (s t f)")
        GW = GN * P
        stage64 = r128[:, 0:GW]
        h2 = r128[:, GW:2 * GW].rearrange("p (t f) -> p t f", t=GN)
        h2T = r128[:, 2 * GW:3 * GW]
        hid = r128[:, 3 * GW:4 * GW]
        x1b = r128[:, 4 * GW:5 * GW].rearrange("p (t f) -> p t f", t=GN)
        y = r128[:, 5 * GW:7 * GW].rearrange("p (b t f) -> p b t f", b=2, t=GN)

        ps_part = psum("ps_part", [P, 2, 512])
        ps_win = psum("ps_win", [P, 2, 512])
        ps_x = psum("ps_x", [P, 4, 512])
        ps_tp, ps_self, ps_out = ps_x[:, 0, :], ps_x[:, 1, :], ps_x[:, 2, :]
        ps_nb, ps_t2, ps_hid = ps_part, ps_win[:, 0, :], ps_win[:, 1, :]

        s_const = sem("s_const")
        s_waits_passed = sem("s_waits_passed")
        s_dve = sem("s_dve")
        s_dst_clear = sem("s_dst_clear")
        s_dst = sem("s_dst")
        s_w = sem("s_w")
        s_wps = sem("s_wps")
        s_wsb = sem("s_wsb")
        s_dstT = sem("s_dstT")
        s_dst_t = sem("s_dst_t")
        s_bcast = sem("s_bcast")
        s_viol = sem("s_viol")
        s_nviol = sem("s_nviol")
        s_npass = sem("s_npass")
        s_clear = sem("s_clear")
        s_load = [sem(f"s_load{i}") for i in range(SLOTS)]
        s_tailz = sem("s_tailz")
        s_onehot = sem("s_onehot")
        s_mm = sem("s_mm")
        s_evac = sem("s_evac")
        s_placed = sem("s_placed")
        s_added = sem("s_added")
        s_pass = sem("s_pass")
        s_xload = sem("s_xload")
        s_bn = sem("s_bn")
        s_mv = sem("s_mv")
        s_std = sem("s_std")
        s_rstd = sem("s_rstd")
        s_nmr = sem("s_nmr")
        s_h = sem("s_h")
        s_tp = sem("s_tp")
        s_ht = sem("s_ht")
        s_self = sem("s_self")
        s_xb = sem("s_xb")
        s_x0 = sem("s_x0")
        s_stage = sem("s_stage")
        s_nb = sem("s_nb")
        s_deg = sem("s_deg")
        s_x1 = sem("s_x1")
        s_bn2 = sem("s_bn2")
        s_mv2 = sem("s_mv2")
        s_std2 = sem("s_std2")
        s_rstd2 = sem("s_rstd2")
        s_nmr2 = sem("s_nmr2")
        s_h2 = sem("s_h2")
        s_t2 = sem("s_t2")
        s_h2t = sem("s_h2t")
        s_hid = sem("s_hid")
        s_hr = sem("s_hr")
        s_o = sem("s_o")
        s_x1b = sem("s_x1b")
        s_y = sem("s_y")
        s_store = [sem(f"s_store{i}") for i in range(2)]

        C_MM, C_EVAC, C_PLACED, C_ADDED = QPI, 2, 2 * QPC, 2
        XL = 16 * (PAIRS + 1)

        block = ctx.enter_context(nc.Block())

        def passes(eng):
            eng.wait_ge(s_npass, 1)
            return eng.value_load(npass[0:1, 0:1], min_val=1, max_val=GEN_PASSES)

        def passes_total(eng):
            return eng.value_load(npass[0:1, 0:1], min_val=1, max_val=GEN_PASSES) * VQ + C_ADDED

        def apart(eng):
            eng.sem_inc(s_waits_passed, 1)

        @block.sync
        def _(sp):
            sp.wait_ge(s_dst_clear, 1)
            full = (TR - 1) * P * P
            rows = (E - full) // P
            sp.dma_start(dst_i[:, 0:TR - 1, :],
                         dst[0:full].rearrange("(c r e) -> r c e", c=TR - 1, r=P)).then_inc(s_dst, 16)
            sp.dma_start(dst_i[0:rows, TR - 1, :],
                         dst[full:full + rows * P].rearrange("(r e) -> r e", e=P)).then_inc(s_dst, 16)
            sp.dma_start(dst_i[rows:rows + 1, TR - 1, 0:E - full - rows * P],
                         dst[full + rows * P:E].rearrange("(r e) -> r e", r=1)).then_inc(s_dst, 16)
            for tile, src in ((ws_raw, W_self), (wn_raw, W_neigh), (wf_raw, W_final), (we_raw, W_edge),
                              (w1a[:], W1[0:D, :]), (w1b[:], W1[D:2 * D, :]), (w2[:], W2),
                              (b0_bc[:], b_final.partition_broadcast(P)), (b2_bc[:], b2.partition_broadcast(P)),
                              (b1_col[:], b1.rearrange("(p o) -> p o", o=1))):
                sp.dma_start(tile, src).then_inc(s_w, 16)

            def load(slot, edge0):
                n = TPC * P
                sp.dma_start(ring128[:, slot, :, :], edge_attr_128[bass.ds(edge0, n), :].rearrange(
                    "(t p) f -> p t f", p=P)).then_inc(s_load[slot], 16)
                sp.dma_start(ring64[:, slot, :, :], edge_attr_64[bass.ds(edge0, n), :].rearrange(
                    "(t p) f -> p t f", p=P)).then_inc(s_load[slot], 16)

            with sp.Fori(0, passes(sp)) as p:
                with sp.Fori(0, TURNS) as it:
                    for c in range(SLOTS):
                        sp.wait_ge(s_mm, p * VQ + it * QPI + (QPC * c + QPC))
                        load(c, it * (QPI * QE) + c * TPC * P)
                        if c == 2:
                            sp.wait_ge(s_x0, p * PAIRS + it + 1)
                            sp.dma_start(xn[:, :, :], x[bass.ds(it * (2 * P), 2 * P), :].rearrange(
                                "(j p) f -> p j f", p=P)).then_inc(s_xload, 16)
                for c in range(SLOTS):
                    if c < SLOTS - 1:
                        sp.wait_ge(s_mm, p * VQ + (TURNS * QPI + QPC * c + QPC))
                        load(c, TURNS * QPI * QE + c * TPC * P)
                    else:
                        sp.wait_ge(s_tailz, p + 1)
                        e0 = (QUADS - 1) * QE
                        whole = TAIL_E // P
                        for ring, src in ((ring128, edge_attr_128), (ring64, edge_attr_64)):
                            sp.dma_start(ring[:, c, 0:whole, :], src[e0:e0 + whole * P, :].rearrange(
                                "(t p) f -> p t f", p=P)).then_inc(s_load[c], 16)
                            sp.dma_start(ring[0:TAIL_E - whole * P, c, whole, :],
                                         src[e0 + whole * P:E, :]).then_inc(s_load[c], 16)
                    if c == 2:
                        sp.wait_ge(s_x0, p * PAIRS + PAIRS)
                        n0 = (NT - 2) * P
                        sp.dma_start(xn[:, 0, :], x[n0:n0 + P, :]).then_inc(s_xload, 16)
                        sp.dma_start(xn[0:LAST_N, 1, :], x[n0 + P:N, :]).then_inc(s_xload, 16)

            for u in range(2):
                sp.sem_inc(s_store[u], 16)
            with sp.Fori(0, GROUPS // 2) as it:
                for u in range(2):
                    sp.wait_ge(s_y, 2 * it + (u + 2))
                    sp.dma_start(out[bass.ds((2 * it + u) * GW, GW), :].rearrange("(j p) f -> p j f", p=P),
                                 y[:, u, :, :]).then_inc(s_store[u], 16)
            g = GROUPS - 1
            sp.wait_ge(s_y, GROUPS + 1)
            for j in range(GN):
                n0 = (g * GN + j) * P
                if n0 < N:
                    n = min(P, N - n0)
                    sp.dma_start(out[n0:n0 + n, :], y[0:n, 0, j, :]).then_inc(s_store[0], 16)
            sp.wait_ge(s_store[0], 16 * (GROUPS // 2 + NT - g * GN) + 16)
            sp.wait_ge(s_store[1], 16 * (GROUPS // 2) + 16)

        @block.gpsimd
        def _(pool):
            nc.gpsimd.memset(ident[:], 0.0).then_inc(s_const, 1)
            nc.gpsimd.memset(ones_f[:], 1.0).then_inc(s_const, 1)
            nc.gpsimd.memset(ones_h[:], 1.0).then_inc(s_const, 1)
            nc.gpsimd.memset(eps[:], EPS).then_inc(s_const, 1)
            nc.gpsimd.memset(w_c[:], 0.0).then_inc(s_const, 1)
            pool.wait_ge(s_const, 5)
            nc.gpsimd.affine_select(out=ident[:], in_=ident[:], compare_op=ALU.not_equal, fill=1.0, base=0,
                                    pattern=[[-1, P]], channel_multiplier=1).then_inc(s_const, 1)
            pool.wait_ge(s_const, 6)
            nc.gpsimd.memset(w_c[D64:D64 + 1, D:D + 1], 1.0).then_inc(s_const, 1)
            pool.wait_ge(s_const, 7)
            nc.gpsimd.iota(iota_win[:], pattern=[[1, PLW]], base=0, channel_multiplier=0,
                           allow_small_or_imprecise_dtypes=True).then_inc(s_const, 1)
            for q in range(TPQ):
                pool.wait_ge(s_const, 8 + q)
                nc.gpsimd.iota(row_in_win[q * WIN:(q + 1) * WIN, :], pattern=[[0, 1]], base=0,
                               channel_multiplier=1, allow_small_or_imprecise_dtypes=True).then_inc(s_const, 1)
            pool.wait_ge(s_const, 12)
            nc.gpsimd.memset(agg[:, 1, :], 0.0).then_inc(s_clear, 1)

            def bias_sum(n, landed):
                pool.wait_ge(s_xload, landed)
                pool.wait_ge(s_x0, n + 1)
                nc.gpsimd.tensor_tensor(xb[:, :, :], xn[:, :, :],
                                        b0_bc[:, :].unsqueeze(1).to_broadcast([P, 2, D]), ALU.add).then_inc(s_xb, 1)

            pool.wait_ge(s_w, 160)
            with pool.Fori(0, passes(pool)) as p:
                with pool.Fori(0, TURNS) as it:
                    bias_sum(p * PAIRS + it, p * XL + it * 16 + 16)
                pool.wait_ge(s_mm, p * VQ + VQ)
                apart(pool)
                whole = TAIL_E // P
                nc.gpsimd.memset(ring128[:, SLOTS - 1, whole:TPQ, :], 0.0)
                nc.gpsimd.memset(ring64[:, SLOTS - 1, whole:TPQ, :], 0.0).then_inc(s_tailz, 1)
                bias_sum(p * PAIRS + (PAIRS - 1), p * XL + XL)

            def stage(g):
                pool.wait_ge(s_nb, g + 1)
                apart(pool)
                nc.gpsimd.tensor_copy(stage64[0:D64 + 1, :], agg[0:D64 + 1, 1, bass.ds(g * GW, GW)]).then_inc(s_stage, 1)

            def add_b2(g):
                pool.wait_ge(s_x1, g + 2)
                pool.wait_ge(s_y, g + 1)
                nc.gpsimd.tensor_tensor(x1b, x0[:, bass.ds(g * GN, GN), :],
                                        b2_bc[:, :].unsqueeze(1).to_broadcast([P, GN, D]), ALU.add).then_inc(s_x1b, 1)

            pool.wait_ge(s_added, passes_total(pool))
            stage(0)
            with pool.Fori(0, GROUPS - 1) as g:
                stage(g + 1)
                add_b2(g)
            add_b2(GROUPS - 1)

        @block.tensor
        def _(pe):
            pe.wait_ge(s_const, 12)
            pe.wait_ge(s_dve, 1)
            for c in range(TR):
                last = nc.tensor.transpose(ps_x[:, c // 4, (c % 4) * P:(c % 4 + 1) * P], dst_f[:, c, :], ident[:])
            last.then_inc(s_dstT, 1)
            pe.wait_ge(s_w, 160)
            for h in range(2):
                last = nc.tensor.transpose(ps_part[:, 0, h * P:(h + 1) * P], wf_raw[:, h * P:(h + 1) * P], ident[:])
            last.then_inc(s_wps, 1)
            pe.wait_ge(s_wsb, 1)
            nc.tensor.matmul(ps_part[:, 1, 0:D], ws_raw, wfT[:, 0, :], start=True, stop=True)
            nc.tensor.matmul(ps_part[:, 1, D:2 * D], wn_raw, wfT[:, 1, :], start=True, stop=True).then_inc(s_wps, 1)
            pe.wait_ge(s_wsb, 2)
            nc.tensor.matmul(ps_part[0:D64, 0, 0:D], we_raw, t1, start=True, stop=True).then_inc(s_wps, 1)
            pe.wait_ge(s_dst_t, 1)
            for b in range(4):
                w = TW // 4
                last = nc.tensor.matmul(ps_x[:, b, 0:w], ones_f[0:1, :], dst_t[0:1, b * w:(b + 1) * w],
                                        start=True, stop=True)
            last.then_inc(s_bcast, 1)
            pe.wait_ge(s_viol, 1)
            nc.tensor.matmul(ps_x[:, 3, 0:1], ones_f[:], nviol[:], start=True, stop=True).then_inc(s_nviol, 1)
            pe.wait_ge(s_clear, 3)
            pe.wait_ge(s_wsb, 3)
            pe.sem_inc(s_mm, C_MM)
            pe.sem_inc(s_placed, C_PLACED)

            def window_sums(slot, q, k, chunk, landed):
                if q == 0:
                    pe.wait_ge(s_load[slot], landed)
                    pe.wait_ge(s_onehot, chunk + 1)
                buf = q % 2
                pe.wait_ge(s_evac, k + 1)
                oh = onehot[:, slot % 2, :, :]
                for t in range(TPQ):
                    rows = slice(t * WIN, (t + 1) * WIN)
                    nc.tensor.matmul(ps_part[rows, buf, 0:D], oh[:, q * TPQ + t, :],
                                     ring128[:, slot, q * TPQ + t, :], start=True, stop=True, tile_position=(0, t * WIN))
                for t in range(TPQ):
                    rows = slice(t * WIN, (t + 1) * WIN)
                    nc.tensor.matmul(ps_part[rows, buf, D:D + D64], oh[:, q * TPQ + t, :],
                                     ring64[:, slot, q * TPQ + t, :], start=True, stop=True, tile_position=(0, t * WIN))
                halves = oh[:, q * TPQ:(q + 1) * TPQ, :].rearrange("p t n -> p (t n)").bitcast(BF16)
                nc.tensor.matmul(ps_part[:, buf, D + D64:D + D64 + 1],
                                 halves.rearrange("p (n h) -> p n h", h=2)[:, :, 1], ones_h[:],
                                 start=True, stop=True).then_inc(s_mm, 1)

            def place_sums(slot, q, k):
                buf = q % 2
                pe.wait_ge(s_evac, k + (1 + C_EVAC))
                pe.wait_ge(s_added, k + 1)
                rhs = place[:, slot % 2, q, :]
                nc.tensor.matmul(ps_win[:, buf, 0:PLW], part[:, buf, 0:D], rhs, start=True, stop=True)
                nc.tensor.matmul(ps_win[0:D64 + 1, buf, PLW:2 * PLW], part[:, buf, D:D + D64 + 1], rhs,
                                 start=True, stop=True).then_inc(s_placed, 1)

            def self_part(step_, n):
                if step_ == 0:
                    pe.wait_ge(s_h, n + 1)
                    for j in range(2):
                        last = nc.tensor.transpose(ps_tp[:, j * P:(j + 1) * P], hn[:, j, :], ident[:])
                    last.then_inc(s_tp, 1)
                else:
                    pe.wait_ge(s_ht, n + 1)
                    pe.wait_ge(s_x0, n + 1)
                    for j in range(2):
                        last = nc.tensor.matmul(ps_self[:, j * D:(j + 1) * D], hT[:, j, :], w_a[:], start=True, stop=True)
                    last.then_inc(s_self, 1)

            def edge_turn(p, it, quads, last):
                k0 = p * VQ + it * QPI
                for i in range(quads):
                    slot, q = i // QPC, i % QPC
                    uses = p * (TURNS + 1) + it
                    landed = uses * 32 + 32
                    if slot == SLOTS - 1:
                        landed = landed + p * 32 + (32 if last else 0)
                    window_sums(slot, q, k0 + i, p * VC + it * SLOTS + slot, landed)
                    if i:
                        place_sums((i - 1) // QPC, (i - 1) % QPC, k0 + i - 1)
                    if i == 3:
                        self_part(0, p * PAIRS + it)
                    if i == 5:
                        self_part(1, p * PAIRS + it)
                place_sums((quads - 1) // QPC, (quads - 1) % QPC, k0 + quads - 1)

            with pe.Fori(0, passes(pe)) as p:
                with pe.Fori(0, TURNS) as it:
                    edge_turn(p, it, QPI, False)
                edge_turn(p, TURNS, LQ, True)
                pe.wait_ge(s_added, p * VQ + (QUADS + C_ADDED))
                pe.sem_inc(s_mm, 1)
                pe.sem_inc(s_placed, 1)

            pe.sem_inc(s_nb, 1)
            pe.sem_inc(s_t2, 1)
            pe.sem_inc(s_hid, 1)
            pe.sem_inc(s_o, 1)
            pe.wait_ge(s_added, passes_total(pe))

            def neigh(g):
                pe.wait_ge(s_stage, g + 1)
                pe.wait_ge(s_x1, g + 1)
                for j in range(GN):
                    o = (j % 2) * (D + 1)
                    last = nc.tensor.matmul(ps_nb[:, j // 2, o:o + D + 1], stage64[0:D64 + 1, j * P:(j + 1) * P], w_c[:],
                                            start=True, stop=True)
                last.then_inc(s_nb, 1)

            def layer1(g, more):
                pe.wait_ge(s_h2, g + 2)
                pe.wait_ge(s_h2t, g + 1)
                for j in range(GN):
                    last = nc.tensor.transpose(ps_t2[:, j * P:(j + 1) * P], h2[:, j, :], ident[:])
                last.then_inc(s_t2, 1)
                if more:
                    neigh(g + 1)
                pe.wait_ge(s_hr, g + 1)
                nc.tensor.matmul(ps_hid, w1b[:], agg[:, 0, bass.ds(g * GW, GW)], start=True, stop=False)
                pe.wait_ge(s_h2t, g + 2)
                nc.tensor.matmul(ps_hid, w1a[:], h2T, start=False, stop=True).then_inc(s_hid, 1)
                pe.wait_ge(s_hr, g + 2)
                pe.wait_ge(s_y, g + 1)
                for j in range(GN):
                    last = nc.tensor.matmul(ps_out[:, j * D:(j + 1) * D], hid[:, j * P:(j + 1) * P], w2[:],
                                            start=True, stop=True)
                last.then_inc(s_o, 1)

            neigh(0)
            with pe.Fori(0, GROUPS - 1) as g:
                layer1(g, True)
            layer1(GROUPS - 1, False)

        @block.scalar
        def _(act):
            act.sem_inc(s_evac, C_EVAC)
            act.wait_ge(s_wps, 1)
            nc.scalar.copy(wfT, ps_part[:, 0, 0:2 * P].rearrange("p (h o) -> p h o", h=2)).then_inc(s_wsb, 1)
            act.wait_ge(s_wps, 2)
            nc.scalar.copy(w_a[:], ps_part[:, 1, 0:D])
            nc.scalar.copy(t1, ps_part[:, 1, D:2 * D]).then_inc(s_wsb, 1)
            act.wait_ge(s_wps, 3)
            act.wait_ge(s_const, 12)
            nc.scalar.copy(w_c[0:D64, 0:D], ps_part[0:D64, 0, 0:D]).then_inc(s_wsb, 1)

            def evacuate(q, k):
                buf = q % 2
                act.wait_ge(s_mm, k + (1 + C_MM))
                act.wait_ge(s_placed, k + (C_PLACED - 1))
                nc.scalar.copy(part[:, buf, 0:D + D64 + 1], ps_part[:, buf, 0:D + D64 + 1]).then_inc(s_evac, 1)

            def ln1(step_, n):
                if step_ == 0:
                    act.wait_ge(s_mv, n + 1)
                    nc.scalar.activation(std[:, 0:2], mv[:, 0:2, 1], ACT.Sqrt, bias=eps[:], scale=1.0).then_inc(s_std, 1)
                elif step_ == 1:
                    act.wait_ge(s_nmr, n + 1)
                    for j in range(2):
                        last = nc.scalar.activation(hn[:, j, :], xn[:, j, :], ACT.Relu, bias=nmr[:, j:j + 1],
                                                    scale=rstd[:, j:j + 1])
                    last.then_inc(s_h, 1)
                else:
                    act.wait_ge(s_tp, n + 1)
                    nc.scalar.copy(hT[:, :, :].rearrange("p j n -> p (j n)"), ps_tp[:, 0:2 * P]).then_inc(s_ht, 1)

            def edge_turn(p, it, quads):
                k0 = p * VQ + it * QPI
                n = p * PAIRS + it
                for i in range(quads):
                    evacuate(i % QPC, k0 + i)
                    if i in (0, 1, 4):
                        ln1((0, 1, 4).index(i), n)

            act.wait_ge(s_const, 12)
            with act.Fori(0, passes(act)) as p:
                with act.Fori(0, TURNS) as it:
                    edge_turn(p, it, QPI)
                edge_turn(p, TURNS, LQ)
                act.wait_ge(s_added, p * VQ + (QUADS + C_ADDED))
                act.sem_inc(s_evac, 1)

            act.sem_inc(s_h2, 1)
            act.sem_inc(s_h2t, 1)
            act.sem_inc(s_hr, 1)

            def norm2(g):
                act.wait_ge(s_mv2, g + 1)
                nc.scalar.activation(std[:, :], mv[:, :, 1], ACT.Sqrt, bias=eps[:], scale=1.0).then_inc(s_std2, 1)
                act.wait_ge(s_nmr2, g + 1)
                act.wait_ge(s_t2, g + 1)
                for j in range(GN):
                    last = nc.scalar.activation(h2[:, j, :], x0[:, bass.ds(g * GN + j, 1), :].rearrange("p o f -> p (o f)"),
                                                ACT.Relu, bias=nmr[:, j:j + 1], scale=rstd[:, j:j + 1])
                last.then_inc(s_h2, 1)

            def turn2(g):
                act.wait_ge(s_t2, g + 2)
                act.wait_ge(s_hid, g + 1)
                nc.scalar.copy(h2T, ps_t2).then_inc(s_h2t, 1)

            def hidden(g):
                act.wait_ge(s_hid, g + 2)
                act.wait_ge(s_o, g + 1)
                nc.scalar.activation(hid, ps_hid, ACT.Relu, bias=b1_col[:], scale=1.0).then_inc(s_hr, 1)

            norm2(0)
            with act.Fori(0, GROUPS - 1) as g:
                turn2(g)
                hidden(g)
                norm2(g + 1)
            turn2(GROUPS - 1)
            hidden(GROUPS - 1)

        @block.vector
        def _(dve):
            own = [0]

            def link(ins):
                own[0] += 1
                ins.then_inc(s_dve, 1)
                dve.wait_ge(s_dve, own[0])

            nc.vector.memset(dst_i[:, TR - 1, :], -1).then_inc(s_dst_clear, 1)
            dve.sem_inc(s_added, C_ADDED)
            dve.sem_inc(s_x0, 1)
            dve.sem_inc(s_x1, 1)
            dve.sem_inc(s_y, 1)
            nc.vector.memset(chk[:], 0.0)
            nc.vector.memset(ps_win[:, :, 0:2 * PLW], 0.0).then_inc(s_clear, 1)
            dve.wait_ge(s_dst, 48)
            link(nc.vector.tensor_copy(dst_f, dst_i))
            nc.vector.memset(agg[:, 0, :], 0.0).then_inc(s_clear, 1)
            nc.vector.memset(rel[:, :], -1.0)
            dve.wait_ge(s_dstT, 1)
            for b in range(4):
                w = min(4 * P, TW - b * 4 * P)
                last = nc.vector.tensor_copy(dst_t[:, b * 4 * P:b * 4 * P + w], ps_x[:, b, 0:w])
            last.then_inc(s_dst_t, 1)
            dve.wait_ge(s_bcast, 1)
            for b in range(4):
                w = TW // 4
                last = nc.vector.tensor_copy(first[:, b * w:(b + 1) * w], ps_x[:, b, 0:w])
            link(last)

            TB = QUADS * TPQ
            f4 = first[:, 0:TB].rearrange("p (k q) -> p k q", q=TPQ)
            nc.vector.tensor_tensor(first_off[:, 0:TB].rearrange("p (k q) -> p k q", q=TPQ), f4,
                                    f4[:, :, 0:1].to_broadcast([P, QUADS, TPQ]), ALU.subtract)
            link(nc.vector.tensor_tensor(rel[:, 0:TB], dst_t[:, 0:TB], first[:, 0:TB], ALU.subtract))
            link(nc.vector.tensor_tensor(place_off[:, 0:TB], rel[:, 0:TB], first_off[:, 0:TB], ALU.add))
            whole, half = E // P, E % P
            tests = ((rel[:, 0:whole], ALU.max, WIN, rel[0:half, whole:TILES]),
                     (place_off[:, 0:whole], ALU.max, PLW, place_off[0:half, whole:TILES]),
                     (dst_t[:, 0:whole], ALU.max, N, dst_t[0:half, whole:TILES]),
                     (rel[:, 0:whole], ALU.min, 0, rel[0:half, whole:TILES]),
                     (first_off[:, 0:TILES], ALU.min, 0, None),
                     (first[:, 0:TILES], ALU.min, 0, None))
            for i, (a, op, _, rest) in enumerate(tests):
                last = nc.vector.tensor_reduce(chk[:, 2 * i:2 * i + 1], a, AX.X, op)
                if rest is not None:
                    last = nc.vector.tensor_copy(chk[0:half, 2 * i + 1:2 * i + 2], rest)
            link(last)
            for i, (_, op, bound, _) in enumerate(tests):
                last = nc.vector.tensor_scalar(viol[:, 2 * i:2 * i + 2], chk[:, 2 * i:2 * i + 2], float(bound), None,
                                               ALU.is_ge if op == ALU.max else ALU.is_lt)
            link(last)
            nc.vector.tensor_reduce(nviol[:], viol[:, 0:2 * len(tests)], AX.X, ALU.add).then_inc(s_viol, 1)
            dve.wait_ge(s_nviol, 1)
            link(nc.vector.tensor_scalar(gen[:], ps_x[:, 3, 0:1], 0.5, None, ALU.is_ge))
            nc.vector.tensor_scalar(npass[0:1, :], gen[0:1, :], float(GEN_PASSES - 1), 1.0, ALU.mult, ALU.add).then_inc(s_npass, 1)
            nc.vector.tensor_scalar(fast[:], gen[:], -1.0, 1.0, ALU.mult, ALU.add)
            link(nc.vector.tensor_scalar(step[:], gen[:], float(WIN), None, ALU.mult))
            link(nc.vector.scalar_tensor_tensor(rel[:, 0:TB], first[:, 0:TB], gen[:, 0:1], rel[:, 0:TB], ALU.mult, ALU.add))
            link(nc.vector.tensor_scalar(rel[:, 0:TB], rel[:, 0:TB], step[:, 0:1], None, ALU.add))
            dve.wait_ge(s_const, 12)
            nc.vector.memset(rowpos[:, QUADS:VQ], -1.0)
            nc.vector.memset(base_f[:, QUADS:VQ], 0.0)
            offs = first_off[:, 0:TB].rearrange("p (k q) -> p k q", q=TPQ)
            for q in range(TPQ):
                r = slice(q * WIN, (q + 1) * WIN)
                nc.vector.tensor_scalar(rowpos[r, 0:QUADS], offs[r, :, q], fast[r, 0:1], row_in_win[r, 0:1], ALU.mult, ALU.add)
            link(nc.vector.tensor_scalar(base_f[0:1, 0:QUADS], f4[0:1, :, 0], fast[0:1, 0:1], step[0:1, 0:1],
                                         ALU.mult, ALU.subtract))

            def one_hots(slot, tile0, quad0, chunk):
                dve.wait_ge(s_placed, chunk * QPC + QPC)
                b = slot % 2
                nc.vector.tensor_tensor(onehot[:, b, :, :], iota_win[:, 0:WIN].unsqueeze(1).to_broadcast([P, TPC, WIN]),
                                        rel[:, bass.ds(tile0, TPC)].unsqueeze(2).to_broadcast([P, TPC, WIN]), ALU.is_equal)
                nc.vector.tensor_tensor(place[:, b, :, :], iota_win[:, :].unsqueeze(1).to_broadcast([P, QPC, PLW]),
                                        rowpos[:, bass.ds(quad0, QPC)].unsqueeze(2).to_broadcast([P, QPC, PLW]),
                                        ALU.is_equal).then_inc(s_onehot, 1)

            def add_sums(q, k, base):
                dve.wait_ge(s_placed, k + (1 + C_PLACED))
                dve.wait_ge(s_added, k + C_ADDED)
                sums = agg[:, :, bass.ds(base, PLW)]
                nc.vector.tensor_tensor(sums, ps_win[:, q % 2, 0:2 * PLW].rearrange("p (a n) -> p a n", a=2), sums,
                                        ALU.add).then_inc(s_added, 1)

            def ln1(step_, n, landed, pair):
                if step_ == 0:
                    dve.wait_ge(s_xload, landed)
                    for j in range(2):
                        last = nc.vector.bn_stats(bn[:, j, :], xn[:, j, :])
                    last.then_inc(s_bn, 1)
                    dve.wait_ge(s_bn, n + 1)
                    apart(dve)
                    for j in range(2):
                        last = nc.vector.bn_aggr(mv[:, j, :], bn[:, j, :])
                    last.then_inc(s_mv, 1)
                elif step_ == 1:
                    dve.wait_ge(s_std, n + 1)
                    nc.vector.reciprocal(rstd[:, 0:2], std[:, 0:2]).then_inc(s_rstd, 1)
                    dve.wait_ge(s_rstd, n + 1)
                    nc.vector.scalar_tensor_tensor(nmr[:, 0:2], mv[:, 0:2, 0], -1.0, rstd[:, 0:2], ALU.mult,
                                                   ALU.mult).then_inc(s_nmr, 1)
                else:
                    dve.wait_ge(s_self, n + 1)
                    dve.wait_ge(s_xb, n + 1)
                    nc.vector.tensor_tensor(x0[:, bass.ds(pair * 2, 2), :],
                                            ps_self[:, 0:2 * D].rearrange("p (j f) -> p j f", j=2), xb[:, :, :],
                                            ALU.add).then_inc(s_x0, 1)

            def edge_turn(p, it, quads, landed):
                k0 = p * VQ + it * QPI
                c0 = p * VC + it * SLOTS
                n = p * PAIRS + it
                one_hots(0, it * (QPI * TPQ), it * QPI, c0)
                one_hots(1, it * (QPI * TPQ) + TPC, it * QPI + QPC, c0 + 1)
                _, bases = nc.values_load_multi_w_load_instructions(
                    base_i[0:1, bass.ds(it * QPI, QPI)], engines=DVE_ONLY, min_val=0, max_val=NPAD - PLW)
                ln1(0, n, landed, it)
                for i in range(quads):
                    add_sums(i % QPC, k0 + i, bases[i])
                    if i % QPC == QPC - 1 and i // QPC + 2 < SLOTS:
                        s = i // QPC + 2
                        one_hots(s, it * (QPI * TPQ) + s * TPC, it * QPI + s * QPC, c0 + s)
                    if i in (0, 6):
                        ln1(1 if i == 0 else 2, n, landed, it)

            with dve.Fori(0, passes(dve)) as p:
                nc.vector.tensor_scalar(base_f[:, :], base_f[:, :], step[0:1, 0:1], None, ALU.add)
                nc.vector.tensor_scalar(rel[:, 0:TB], rel[:, 0:TB], step[:, 0:1], None, ALU.subtract).then_inc(s_pass, 1)
                dve.wait_ge(s_pass, 3 * p + 1)
                nc.vector.tensor_copy(base_i[:, :], base_f[:, :]).then_inc(s_pass, 1)
                dve.wait_ge(s_pass, 3 * p + 2)
                apart(dve)
                with dve.Fori(0, TURNS) as it:
                    edge_turn(p, it, QPI, p * XL + it * 16 + 16)
                edge_turn(p, TURNS, LQ, p * XL + XL)
                dve.wait_ge(s_added, p * VQ + (QUADS + C_ADDED))
                dve.sem_inc(s_added, 1)
                dve.sem_inc(s_pass, 1)

            nc.vector.memset(x0[:, NT:GROUPS * GN, :], 0.0).then_inc(s_deg, 1)
            dve.wait_ge(s_deg, 1)

            def x_after_layer0(g):
                dve.wait_ge(s_nb, g + 2)
                nb = ps_nb[:, :, 0:2 * (D + 1)].rearrange("p b (t c) -> p b t c", t=2)
                nc.vector.tensor_scalar(deg[:, :].rearrange("p (b t) -> p b t", b=2), nb[:, :, :, D], 1.0, None,
                                        ALU.max).then_inc(s_deg, 1)
                dve.wait_ge(s_deg, 2 * g + 2)
                nc.vector.reciprocal(rdeg[:, :], deg[:, :]).then_inc(s_deg, 1)
                dve.wait_ge(s_deg, 2 * g + 3)
                for j in range(GN):
                    row = x0[:, bass.ds(g * GN + j, 1), :].rearrange("p o f -> p (o f)")
                    last = nc.vector.scalar_tensor_tensor(row, nb[:, j // 2, j % 2, 0:D], rdeg[:, j:j + 1], row,
                                                          ALU.mult, ALU.add)
                last.then_inc(s_x1, 1)
                dve.wait_ge(s_x1, g + 2)
                apart(dve)
                for j in range(GN):
                    last = nc.vector.bn_stats(bn[:, j, :], x0[:, bass.ds(g * GN + j, 1), :].rearrange("p o f -> p (o f)"))
                last.then_inc(s_bn2, 1)
                dve.wait_ge(s_bn2, g + 1)
                apart(dve)
                for j in range(GN):
                    last = nc.vector.bn_aggr(mv[:, j, :], bn[:, j, :])
                last.then_inc(s_mv2, 1)
                dve.wait_ge(s_std2, g + 1)
                nc.vector.reciprocal(rstd[:, :], std[:, :]).then_inc(s_rstd2, 1)
                dve.wait_ge(s_rstd2, g + 1)
                dve.wait_ge(s_h2, g + 1)
                nc.vector.scalar_tensor_tensor(nmr[:, :], mv[:, :, 0], -1.0, rstd[:, :], ALU.mult,
                                               ALU.mult).then_inc(s_nmr2, 1)

            def result(g, u, stored):
                dve.wait_ge(s_o, g + 2)
                dve.wait_ge(s_x1b, g + 1)
                dve.wait_ge(s_store[u], stored)
                nc.vector.tensor_tensor(y[:, u, :, :], ps_out.rearrange("p (t f) -> p t f", t=GN), x1b, ALU.add).then_inc(s_y, 1)

            x_after_layer0(0)
            with dve.Fori(0, GROUPS // 2) as it:
                for u in range(2):
                    x_after_layer0(2 * it + (u + 1))
                    result(2 * it + u, u, 16 * it + 16)
            result(GROUPS - 1, 0, 16 * (GROUPS // 2) + 16)


_USED = ['x', 'dst', 'edge_attr_128', 'edge_attr_64', 'L0_gnn_W_self', 'L0_gnn_W_neigh', 'L0_gnn_W_edge',
         'L0_gnn_W_final', 'L0_gnn_b_final', 'L1_gnn_W1', 'L1_gnn_b1', 'L1_gnn_W2', 'L1_gnn_b2']


def kernel(**inputs):
    import numpy as _np
    import concourse.bacc as _bacc
    from concourse import mybir as _mybir
    from concourse.bass_utils import run_bass_kernel_spmd as _run

    nc = _bacc.Bacc("TRN2", target_bir_lowering=False, num_devices=1)
    arrays, args = {}, []
    for name in _USED:
        a = _np.ascontiguousarray(inputs[name])
        arrays[f"in_{name}_dram"] = a
        args.append(nc.dram_tensor(f"in_{name}_dram", a.shape, _mybir.dt.from_np(a.dtype), kind="ExternalInput").ap())
    args.append(nc.dram_tensor("out_0_dram", inputs['x'].shape, _mybir.dt.float32, kind="ExternalOutput").ap())
    build_gnn(nc, *args)
    r = _run(nc, [arrays], core_ids=[0])
    return r.results[0]["out_0_dram"]
```

```python
from contextlib import ExitStack

import concourse.bass as bass
from concourse import mybir

F32 = mybir.dt.float32
BF16 = mybir.dt.bfloat16
I16 = mybir.dt.int16
I32 = mybir.dt.int32
ALU = mybir.AluOpType
ACT = mybir.ActivationFunctionType
AX = mybir.AxisListType
DVE_ONLY = [mybir.EngineType.DVE]

P = 128
EPS = 1e-5


def build_gnn(nc, x, dst, edge_attr_128, edge_attr_64, W_self, W_neigh, W_edge, W_final, b_final,
              W1, b1, W2, b2, out):
    N, D = x.shape
    E = dst.shape[0]
    D64 = edge_attr_64.shape[1]
    H = P // 2
    assert D == P and D64 == H

    WIN = 64
    RUN = 3
    BE = RUN * P
    BPC = 2
    SLOTS = 5
    AHEAD = 3
    BATCHES = -(-E // BE)
    CHUNKS = -(-BATCHES // BPC)
    TURNS = CHUNKS // SLOTS
    BPT = BPC * SLOTS
    CE = BPC * BE
    LAST_E = E - (BATCHES - 1) * BE
    LAST_R = LAST_E // RUN
    assert CHUNKS == TURNS * SLOTS + 1 and BATCHES % BPC == 1 and LAST_E > LAST_R * RUN
    ROUNDS = -(-BATCHES // P)
    ROWS = BATCHES - (ROUNDS - 1) * P

    NT = -(-N // P)
    GN = 4
    GROUPS = -(-NT // GN)
    GW = GN * P
    NPAD = GROUPS * GW
    LAST_N = N - (NT - 1) * P
    PAIRS = NT // 2
    assert PAIRS * 2 == NT and PAIRS + 1 <= TURNS and GROUPS % 2 == 1 and GROUPS >= 3
    GEN_PASSES = -(-N // WIN)
    assert GEN_PASSES * WIN <= NPAD and N <= NPAD - WIN

    with ExitStack() as ctx:
        def sb(name, shape, dt=F32):
            return ctx.enter_context(nc.sbuf_tensor(name, shape, dt))

        def psum(name, shape):
            return ctx.enter_context(nc.psum_tensor(name, shape, F32))

        def sem(name):
            return ctx.enter_context(nc.semaphore(name))

        agg = sb("agg", [P, 2, NPAD])
        x0 = sb("x0", [P, GROUPS * GN, D])
        ring128 = sb("ring128", [P, SLOTS, BPC, RUN * D])
        ring64 = sb("ring64", [P, SLOTS, BPC, RUN * D64])
        rel = sb("rel", [P, CHUNKS * BPC, RUN])
        base = sb("base", [1, CHUNKS * BPC], I16)
        base_pair = base[0:1, :].bitcast(I32)
        onehot = sb("onehot", [P, SLOTS, BPC * RUN, WIN])
        xn = sb("xn", [P, 2, D])
        xb = sb("xb", [P, 2, D])
        hn = sb("hn", [P, 2, D])
        hT = sb("hT", [P, 2, P])
        w_a = sb("w_a", [P, D])
        w_c = sb("w_c", [P, D + 1])
        w1a = sb("w1a", [P, D])
        w1b = sb("w1b", [P, D])
        w2 = sb("w2", [P, D])
        b0_bc = sb("b0_bc", [P, D])
        b2_bc = sb("b2_bc", [P, D])
        b1_col = sb("b1_col", [P, 1])
        ident = sb("ident", [P, P])
        ones_f = sb("ones_f", [P, P])
        ones_h = sb("ones_h", [P, H], BF16)
        iota_win = sb("iota_win", [P, WIN])
        eps = sb("eps", [P, 1])
        bn = sb("bn", [P, GN, 6])
        mv = sb("mv", [P, 2, GN, 2])
        std = sb("std", [P, 2, GN])
        rstd = sb("rstd", [P, 2, GN])
        nmr = sb("nmr", [P, 2, GN])
        deg = sb("deg", [P, GN])
        rdeg = sb("rdeg", [P, GN])
        chk = sb("chk", [P, 8])
        nviol = sb("nviol", [P, 1])
        gen = sb("gen", [1, 1], I32)

        flat = x0[:, :, :].rearrange("p t f -> p (t f)")
        at = [0]

        def scratch(cols):
            at[0] += cols
            assert at[0] <= NPAD
            return flat[:, at[0] - cols:at[0]]

        dst_i = scratch(ROUNDS * BE).bitcast(I32).rearrange("p (c e) -> p c e", c=ROUNDS)
        rel_f = scratch(ROUNDS * BE).rearrange("p (c e) -> p c e", c=ROUNDS)
        firsts = scratch(ROUNDS)
        ws_raw, wn_raw, we_raw = scratch(D), scratch(D), scratch(D64)
        wf_raw = scratch(2 * D)
        wfT = scratch(2 * D).rearrange("p (h o) -> p h o", h=2)
        t1 = scratch(D)

        r128 = ring128[:, :, :, :].rearrange("p s b f -> p (s b f)")
        stage64 = r128[:, 0:2 * GW].rearrange("p (b n) -> p b n", b=2)
        h2 = r128[:, 2 * GW:4 * GW].rearrange("p (b t f) -> p b t f", b=2, t=GN)
        x1b = r128[:, 4 * GW:6 * GW].rearrange("p (b t f) -> p b t f", b=2, t=GN)
        h2T = r128[:, 6 * GW:7 * GW]
        r64 = ring64[:, :, :, :].rearrange("p s b f -> p (s b f)")
        y = r64[:, 0:2 * GW].rearrange("p (b t f) -> p b t f", b=2, t=GN)
        hid = r64[:, 2 * GW:3 * GW]

        ps = psum("ps", [P, 8, 512])
        ps_sum = ps[:, 0:SLOTS, :]
        ps_tp, ps_self = ps[:, 5, :], ps[:, 6, :]
        ps_tab = ps[:, 0:4, :].rearrange("p b n -> p (b n)")
        ps_base = ps[0:1, 5:7, :].rearrange("p b n -> p (b n)")
        ps_w, ps_viol = ps[:, 7, :], ps[:, 4, 0:1]
        ps_nb = (ps[:, 0:2, :], ps[:, 2:4, :])
        ps_t2, ps_hid = ps[:, 4, :], ps[:, 7, :]
        ps_out = (ps[:, 5, :], ps[:, 6, :])

        s_const = sem("s_const")
        s_waits_passed = sem("s_waits_passed")
        s_dve = sem("s_dve")
        s_dst_clear = sem("s_dst_clear")
        s_dst = sem("s_dst")
        s_relf = sem("s_relf")
        s_turn = sem("s_turn")
        s_untab = sem("s_untab")
        s_pool_clear = sem("s_pool_clear")
        s_w = sem("s_w")
        s_wps = sem("s_wps")
        s_wsb = sem("s_wsb")
        s_viol = sem("s_viol")
        s_nviol = sem("s_nviol")
        s_gen = sem("s_gen")
        s_load = [sem(f"s_load{i}") for i in range(SLOTS)]
        s_onehot = sem("s_onehot")
        s_mm = sem("s_mm")
        s_added = sem("s_added")
        s_pass = sem("s_pass")
        s_xload = sem("s_xload")
        s_bn, s_mv, s_std, s_rstd, s_nmr = (sem(n) for n in ("s_bn", "s_mv", "s_std", "s_rstd", "s_nmr"))
        s_h, s_tp, s_ht, s_self, s_xb, s_x0 = (sem(n) for n in ("s_h", "s_tp", "s_ht", "s_self", "s_xb", "s_x0"))
        s_stage, s_nb, s_deg, s_x1 = (sem(n) for n in ("s_stage", "s_nb", "s_deg", "s_x1"))
        s_bn2, s_mv2, s_std2, s_rstd2, s_nmr2 = (sem(n) for n in ("s_bn2", "s_mv2", "s_std2", "s_rstd2", "s_nmr2"))
        s_h2, s_t2, s_h2t, s_hid, s_hr = (sem(n) for n in ("s_h2", "s_t2", "s_h2t", "s_hid", "s_hr"))
        s_o, s_x1b, s_y = (sem(n) for n in ("s_o", "s_x1b", "s_y"))
        s_store = [sem(f"s_store{i}") for i in range(2)]

        C_MM, C_ADDED = SLOTS, BPT
        XL = 16 * (PAIRS + 1)
        N_CONST = 9
        WARM_UP = 24
        KEEPERS = 2

        block = ctx.enter_context(nc.Block())

        def general(eng):
            eng.wait_ge(s_gen, 1)
            return eng.value_load(gen[0:1, 0:1], min_val=0, max_val=1)

        def all_passes(eng, run_pass, setup=None):
            run_pass(0)
            again = general(eng)
            with eng.If(again > 0):
                if setup is not None:
                    setup()
                with eng.Fori(1, GEN_PASSES + 1) as p:
                    run_pass(p)
            return again * (GEN_PASSES * BATCHES) + (BATCHES + C_ADDED)

        def turns(eng, turn):
            turn(0, finish=False)
            with eng.Fori(1, PAIRS - 1) as it:
                turn(it)
            turn(PAIRS - 1)
            turn(PAIRS, start=False)
            for it in range(PAIRS + 1, TURNS):
                turn(it, start=False, finish=False)

        def landed(p, it, slot):
            return p * (32 * TURNS + (64 if slot == 0 else 0)) + it * 32 + (64 if isinstance(it, int) and it == TURNS else 32)

        def apart(eng):
            eng.sem_inc(s_waits_passed, 1)

        @block.sync
        def _(sp):
            def load_dst(times):
                sp.wait_ge(s_dst_clear, times)
                full = (ROUNDS - 1) * P * BE
                whole = (ROWS - 1) * BE
                sp.dma_start(dst_i[:, 0:ROUNDS - 1, :],
                             dst[0:full].rearrange("(c r e) -> r c e", c=ROUNDS - 1, r=P)).then_inc(s_dst, 16)
                sp.dma_start(dst_i[0:ROWS - 1, ROUNDS - 1, :],
                             dst[full:full + whole].rearrange("(r e) -> r e", e=BE)).then_inc(s_dst, 16)
                sp.dma_start(dst_i[ROWS - 1:ROWS, ROUNDS - 1, 0:LAST_E],
                             dst[E - LAST_E:E].rearrange("(r e) -> r e", r=1)).then_inc(s_dst, 16)

            def run_pass(p):
                if not isinstance(p, int):
                    sp.wait_ge(s_mm, p * CHUNKS + C_MM)
                    apart(sp)

                with sp.Fori(0, TURNS) as it:
                    for c in range(SLOTS):
                        sp.wait_ge(s_mm, p * CHUNKS + it * SLOTS + (c + 1))
                        edges = bass.ds(it * (SLOTS * CE) + c * CE, CE)
                        sp.dma_start(ring128[:, c, :, :], edge_attr_128[edges, :].rearrange(
                            "(b p r) f -> p b (r f)", p=P, r=RUN)).then_inc(s_load[c], 16)
                        sp.dma_start(ring64[:, c, :, :], edge_attr_64[edges, :].rearrange(
                            "(b p r) f -> p b (r f)", p=P, r=RUN)).then_inc(s_load[c], 16)

                sp.wait_ge(s_mm, p * CHUNKS + TURNS * SLOTS + 1)
                e0 = (BATCHES - 1) * BE
                e1 = e0 + LAST_R * RUN
                for ring, feats, w in ((ring128, edge_attr_128, D), (ring64, edge_attr_64, D64)):
                    sp.dma_start(ring[0:LAST_R, 0, 0, :], feats[e0:e1, :].rearrange(
                        "(p r) f -> p (r f)", r=RUN)).then_inc(s_load[0], 16)
                    sp.dma_start(ring[LAST_R:LAST_R + 1, 0, 0, 0:(E - e1) * w], feats[e1:E, :].rearrange(
                        "(p r) f -> p (r f)", p=1)).then_inc(s_load[0], 16)

            load_dst(1)
            all_passes(sp, run_pass, lambda: load_dst(2))

            for u in range(2):
                sp.sem_inc(s_store[u], 16)
            with sp.Fori(0, GROUPS // 2) as it:
                for u in range(2):
                    sp.wait_ge(s_y, 2 * it + (u + 3))
                    sp.dma_start(out[bass.ds((2 * it + u) * GW, GW), :].rearrange("(j p) f -> p j f", p=P),
                                 y[:, u, :, :]).then_inc(s_store[u], 16)
            g = GROUPS - 1
            sp.wait_ge(s_y, GROUPS + 2)
            for j in range(GN):
                n0 = (g * GN + j) * P
                if n0 < N:
                    n = min(P, N - n0)
                    sp.dma_start(out[n0:n0 + n, :], y[0:n, 0, j, :]).then_inc(s_store[0], 16)
            sp.wait_ge(s_store[0], 16 * (GROUPS // 2 + NT - g * GN) + 16)
            sp.wait_ge(s_store[1], 16 * (GROUPS // 2) + 16)

        @block.gpsimd
        def _(pool):
            own = [0]

            def const(ins):
                own[0] += 1
                ins.then_inc(s_const, 1)
                pool.wait_ge(s_const, own[0])

            const(nc.gpsimd.memset(ident[:], 0.0))
            const(nc.gpsimd.affine_select(out=ident[:], in_=ident[:], compare_op=ALU.not_equal, fill=1.0, base=0,
                                          pattern=[[-1, P]], channel_multiplier=1))
            const(nc.gpsimd.iota(iota_win[:], pattern=[[1, WIN]], base=0, channel_multiplier=0,
                                 allow_small_or_imprecise_dtypes=True))
            const(nc.gpsimd.memset(ones_h[:], 1.0))
            const(nc.gpsimd.memset(ones_f[:], 1.0))
            const(nc.gpsimd.memset(eps[:], EPS))
            const(nc.gpsimd.memset(chk[:], 0.0))
            const(nc.gpsimd.memset(w_c[:], 0.0))
            const(nc.gpsimd.memset(w_c[0:1, D:D + 1], 1.0))
            assert own[0] == N_CONST
            nc.gpsimd.memset(agg[:, 0, :], 0.0)
            nc.gpsimd.memset(agg[:, 1, :], 0.0).then_inc(s_pool_clear, 1)

            def run_pass(p):
                def turn(it):
                    pool.wait_ge(s_xload, p * XL + (XL if isinstance(it, int) else it * 16 + 16))
                    pool.wait_ge(s_x0, p * PAIRS + it + 1)
                    nc.gpsimd.tensor_tensor(xb[:, :, :], xn[:, :, :],
                                            b0_bc[:, :].unsqueeze(1).to_broadcast([P, 2, D]), ALU.add).then_inc(s_xb, 1)

                with pool.Fori(0, PAIRS - 1) as it:
                    turn(it)
                turn(PAIRS - 1)

            pool.wait_ge(s_w, 160)
            done = all_passes(pool, run_pass)

            def stage(g, u):
                pool.wait_ge(s_nb, g + 1)
                apart(pool)
                nc.gpsimd.tensor_copy(stage64[:, u, :], agg[:, 1, bass.ds(g * GW, GW)]).then_inc(s_stage, 1)

            def add_b2(g, u):
                pool.wait_ge(s_x1, g + 3)
                pool.wait_ge(s_y, g + 1)
                nc.gpsimd.tensor_tensor(x1b[:, u, :, :], x0[:, bass.ds(g * GN, GN), :],
                                        b2_bc[:, :].unsqueeze(1).to_broadcast([P, GN, D]), ALU.add).then_inc(s_x1b, 1)

            pool.wait_ge(s_added, done)
            stage(0, 0)
            stage(1, 1)
            with pool.Fori(0, GROUPS // 2 - 1) as it:
                for u in range(2):
                    stage(2 * it + (u + 2), u)
                    add_b2(2 * it + u, u)
            stage(GROUPS - 1, 0)
            for g in range(GROUPS - 3, GROUPS):
                add_b2(g, g % 2)

        @block.tensor
        def _(pe):
            def turn_tables(times):
                pe.wait_ge(s_relf, times)
                for r in range(RUN):
                    for c in range(ROUNDS):
                        k = r * ROUNDS + c
                        last = nc.tensor.transpose(ps_tab[:, k * P:(k + 1) * P],
                                                   rel_f[:, c, :].rearrange("b (p r) -> b r p", r=RUN)[:, r, :], ident[:])
                last.then_inc(s_turn, 1)

            pe.wait_ge(s_const, N_CONST)
            turn_tables(1)
            for c in range(ROUNDS):
                last = nc.tensor.matmul(ps_base[:, c * P:(c + 1) * P], firsts[:, c:c + 1], ident[:], start=True, stop=True)
            last.then_inc(s_turn, 1)
            pe.sem_inc(s_mm, C_MM)
            pe.wait_ge(s_w, 160)
            for h in range(2):
                last = nc.tensor.transpose(ps_w[:, h * P:(h + 1) * P], wf_raw[:, h * P:(h + 1) * P], ident[:])
            last.then_inc(s_wps, 1)
            pe.wait_ge(s_wsb, 1)
            nc.tensor.matmul(ps_w[:, 0:D], ws_raw, wfT[:, 0, :], start=True, stop=True)
            nc.tensor.matmul(ps_w[:, D:2 * D], wn_raw, wfT[:, 1, :], start=True, stop=True).then_inc(s_wps, 1)
            pe.wait_ge(s_wsb, 2)
            nc.tensor.matmul(ps_w[H:P, 0:D], we_raw, t1, start=True, stop=True).then_inc(s_wps, 1)
            pe.wait_ge(s_viol, 1)
            nc.tensor.matmul(ps_viol, ones_f[:], nviol[:], start=True, stop=True).then_inc(s_nviol, 1)
            pe.wait_ge(s_untab, 2)
            pe.wait_ge(s_gen, 1)
            pe.wait_ge(s_wsb, 3)
            for i in range(WARM_UP):
                nc.tensor.matmul(ps_w[:, 0:P], ones_f[:], ident[:], start=True, stop=True)

            def sums(slot, batches, chunk, j, load):
                pe.wait_ge(s_load[slot], load)
                pe.wait_ge(s_onehot, chunk + 1)
                pe.wait_ge(s_added, j)
                hots = onehot[:, slot, :, :].rearrange("p (b r) n -> p b r n", r=RUN)
                halves = onehot[:, slot, :, :].bitcast(BF16).rearrange("p (b r) (n h) -> p b r n h", r=RUN, h=2)
                totals = ps_sum[:, slot, 0:BPC * 2 * WIN].rearrange("p (b a n) -> p b a n", b=BPC, a=2)
                for b in range(batches):
                    for r in range(RUN):
                        first, final = r == 0, r == RUN - 1
                        nc.tensor.matmul(totals[0:H, b, 0, :], ring128[:, slot, b, r * D:r * D + H], hots[:, b, r, :],
                                         start=first, stop=final)
                        nc.tensor.matmul(totals[H:P, b, 0, :], ring128[:, slot, b, r * D + H:(r + 1) * D], hots[:, b, r, :],
                                         start=first, stop=final)
                for b in range(batches):
                    for r in range(RUN):
                        nc.tensor.matmul(totals[H:P, b, 1, :], ring64[:, slot, b, r * D64:(r + 1) * D64], hots[:, b, r, :],
                                         start=r == 0, stop=r == RUN - 1)
                for i in range(KEEPERS):
                    nc.tensor.matmul(ps_w[0:H, :], ones_h[:], onehot[:, slot, :, :].bitcast(BF16).rearrange("p t n -> p (t n)")[:, 0:512],
                                     start=True, stop=True)
                for r in range(RUN):
                    last = nc.tensor.matmul(totals[0:H, 0:batches, 1, :], ones_h[:], halves[:, 0:batches, r, :, 1],
                                            start=r == 0, stop=r == RUN - 1)
                last.then_inc(s_mm, 1)

            def self_part(step, n):
                if step == 0:
                    pe.wait_ge(s_h, n + 1)
                    for j in range(2):
                        last = nc.tensor.transpose(ps_tp[:, j * P:(j + 1) * P], hn[:, j, :], ident[:])
                    last.then_inc(s_tp, 1)
                else:
                    pe.wait_ge(s_ht, n + 1)
                    pe.wait_ge(s_x0, n + 1)
                    for j in range(2):
                        last = nc.tensor.matmul(ps_self[:, j * D:(j + 1) * D], hT[:, j, :], w_a[:], start=True, stop=True)
                    last.then_inc(s_self, 1)

            def run_pass(p):
                def turn(it, start=True, finish=True):
                    if finish:
                        self_part(0, p * PAIRS + it - 1)
                    for c in range(SLOTS):
                        sums(c, BPC, p * CHUNKS + it * SLOTS + c, p * BATCHES + it * BPT + (c + 1) * BPC, landed(p, it, c))
                        if finish and c == 0:
                            self_part(1, p * PAIRS + it - 1)

                turns(pe, turn)
                sums(0, 1, p * CHUNKS + TURNS * SLOTS, p * BATCHES + TURNS * BPT + 1, landed(p, TURNS, 0))
                pe.wait_ge(s_added, p * BATCHES + (BATCHES + C_ADDED))
                apart(pe)

            def setup():
                turn_tables(2)
                pe.wait_ge(s_untab, 3)

            done = all_passes(pe, run_pass, setup)

            for s in (s_nb, s_o):
                pe.sem_inc(s, 2)
            for s in (s_t2, s_hid):
                pe.sem_inc(s, 1)
            pe.wait_ge(s_added, done)

            def neigh(g, u):
                pe.wait_ge(s_stage, g + 1)
                pe.wait_ge(s_x1, g + 1)
                for j in range(GN):
                    o = (j % 2) * (D + 1)
                    last = nc.tensor.matmul(ps_nb[u][:, j // 2, o:o + D + 1], stage64[:, u, j * P:(j + 1) * P],
                                            w_c[:], start=True, stop=True)
                last.then_inc(s_nb, 1)

            def layer1(g, u, more):
                pe.wait_ge(s_h2, g + 2)
                pe.wait_ge(s_h2t, g + 1)
                for j in range(GN):
                    last = nc.tensor.transpose(ps_t2[:, j * P:(j + 1) * P], h2[:, u, j, :], ident[:])
                last.then_inc(s_t2, 1)
                pe.wait_ge(s_hr, g + 1)
                nc.tensor.matmul(ps_hid, w1b[:], agg[:, 0, bass.ds(g * GW, GW)], start=True, stop=False)
                if more:
                    neigh(g + 2, u)
                pe.wait_ge(s_h2t, g + 2)
                nc.tensor.matmul(ps_hid, w1a[:], h2T, start=False, stop=True).then_inc(s_hid, 1)
                pe.wait_ge(s_hr, g + 2)
                pe.wait_ge(s_y, g + 1)
                for j in range(GN):
                    last = nc.tensor.matmul(ps_out[u][:, j * D:(j + 1) * D], hid[:, j * P:(j + 1) * P], w2[:],
                                            start=True, stop=True)
                last.then_inc(s_o, 1)

            neigh(0, 0)
            neigh(1, 1)
            with pe.Fori(0, GROUPS // 2 - 1) as it:
                for u in range(2):
                    layer1(2 * it + u, u, True)
            for g in range(GROUPS - 3, GROUPS):
                layer1(g, g % 2, g + 2 < GROUPS)

        @block.scalar
        def _(act):
            for tile, src in ((ws_raw, W_self), (wn_raw, W_neigh), (wf_raw, W_final), (we_raw, W_edge),
                              (w1a[:], W1[0:D, :]), (w1b[:], W1[D:2 * D, :]), (w2[:], W2),
                              (b0_bc[:], b_final.partition_broadcast(P)), (b2_bc[:], b2.partition_broadcast(P)),
                              (b1_col[:], b1.rearrange("(p o) -> p o", o=1))):
                act.dma_start(tile, src).then_inc(s_w, 16)
            act.wait_ge(s_wps, 1)
            nc.scalar.copy(wfT, ps_w[:, 0:2 * P].rearrange("p (h o) -> p h o", h=2)).then_inc(s_wsb, 1)
            act.wait_ge(s_wps, 2)
            nc.scalar.copy(w_a[:], ps_w[:, 0:D])
            nc.scalar.copy(t1, ps_w[:, D:2 * D]).then_inc(s_wsb, 1)
            act.wait_ge(s_wps, 3)
            act.wait_ge(s_const, N_CONST)
            nc.scalar.copy(w_c[H:P, 0:D], ps_w[H:P, 0:D]).then_inc(s_wsb, 1)

            def load_x(pair):
                if isinstance(pair, int) and pair == PAIRS - 1:
                    n0 = pair * 2 * P
                    act.dma_start(xn[:, 0, :], x[n0:n0 + P, :]).then_inc(s_xload, 16)
                    act.dma_start(xn[0:LAST_N, 1, :], x[n0 + P:N, :]).then_inc(s_xload, 16)
                else:
                    act.dma_start(xn[:, :, :], x[bass.ds(pair * (2 * P), 2 * P), :].rearrange(
                        "(j p) f -> p j f", p=P)).then_inc(s_xload, 16)

            def run_pass(p):
                def turn(it):
                    n = p * PAIRS + it
                    act.wait_ge(s_mv, n + 1)
                    nc.scalar.activation(std[:, 0, 0:2], mv[:, 0, 0:2, 1], ACT.Sqrt, bias=eps[:], scale=1.0).then_inc(s_std, 1)
                    act.wait_ge(s_nmr, n + 1)
                    for j in range(2):
                        last = nc.scalar.activation(hn[:, j, :], xn[:, j, :], ACT.Relu, bias=nmr[:, 0, j:j + 1],
                                                    scale=rstd[:, 0, j:j + 1])
                    last.then_inc(s_h, 1)
                    if not (isinstance(it, int) and it == PAIRS - 1):
                        act.wait_ge(s_h, n + 1)
                        apart(act)
                        act.wait_ge(s_xb, n + 2)
                        apart(act)
                        load_x(it + 1)
                    act.wait_ge(s_tp, n + 1)
                    nc.scalar.copy(hT[:, :, :].rearrange("p j n -> p (j n)"), ps_tp[:, 0:2 * P]).then_inc(s_ht, 1)

                if not isinstance(p, int):
                    act.wait_ge(s_xb, p * PAIRS + 1)
                    apart(act)
                load_x(0)
                with act.Fori(0, PAIRS - 2) as it:
                    turn(it)
                turn(PAIRS - 2)
                turn(PAIRS - 1)

            done = all_passes(act, run_pass)

            for s in (s_h2, s_h2t, s_hr):
                act.sem_inc(s, 1)
            act.wait_ge(s_added, done)

            def norm2(g, u):
                act.wait_ge(s_mv2, g + 1)
                nc.scalar.activation(std[:, u, :], mv[:, u, :, 1], ACT.Sqrt, bias=eps[:], scale=1.0).then_inc(s_std2, 1)
                act.wait_ge(s_nmr2, g + 1)
                for j in range(GN):
                    last = nc.scalar.activation(h2[:, u, j, :], x0[:, bass.ds(g * GN + j, 1), :].rearrange("p o f -> p (o f)"),
                                                ACT.Relu, bias=nmr[:, u, j:j + 1], scale=rstd[:, u, j:j + 1])
                last.then_inc(s_h2, 1)

            def turn2(g):
                act.wait_ge(s_t2, g + 2)
                act.wait_ge(s_hid, g + 1)
                nc.scalar.copy(h2T, ps_t2).then_inc(s_h2t, 1)

            def hidden(g):
                act.wait_ge(s_hid, g + 2)
                act.wait_ge(s_o, g + 2)
                nc.scalar.activation(hid, ps_hid, ACT.Relu, bias=b1_col[:], scale=1.0).then_inc(s_hr, 1)

            norm2(0, 0)
            norm2(1, 1)
            with act.Fori(0, GROUPS // 2 - 1) as it:
                for u in range(2):
                    turn2(2 * it + u)
                    hidden(2 * it + u)
                    norm2(2 * it + (u + 2), u)
            for g in range(GROUPS - 3, GROUPS):
                turn2(g)
                hidden(g)
                if g + 2 < GROUPS:
                    norm2(g + 2, g % 2)

        @block.vector
        def _(dve):
            own = [0]

            def link(ins):
                own[0] += 1
                ins.then_inc(s_dve, 1)
                dve.wait_ge(s_dve, own[0])

            def copy_table():
                nc.vector.tensor_copy(rel[:, :, :].rearrange("p b r -> p r b"),
                                      ps_tab[:, 0:RUN * ROUNDS * P].rearrange("p (r b) -> p r b", r=RUN)[:, :, 0:CHUNKS * BPC]
                                      ).then_inc(s_untab, 1)

            nc.vector.memset(dst_i[:, ROUNDS - 1, :], -1).then_inc(s_dst_clear, 1)
            dve.sem_inc(s_added, C_ADDED)
            for s in (s_x0, s_xb):
                dve.sem_inc(s, 1)
            for s in (s_x1, s_y):
                dve.sem_inc(s, 2)
            dve.wait_ge(s_dst, 48)
            nc.vector.tensor_copy(firsts, dst_i[:, :, 0])
            nc.vector.tensor_tensor(rel_f, dst_i, dst_i[:, :, 0:1].to_broadcast([P, ROUNDS, BE]), ALU.subtract).then_inc(s_relf, 1)
            dve.wait_ge(s_turn, 1)
            copy_table()
            dve.wait_ge(s_turn, 2)
            nc.vector.tensor_scalar(base[0:1, :], ps_base[:, 0:CHUNKS * BPC], 0.0, float(NPAD - WIN), ALU.max,
                                    ALU.min).then_inc(s_untab, 1)

            def check():
                c = ROUNDS - 1
                dve.wait_ge(s_const, N_CONST)
                nc.vector.tensor_reduce(chk[:, 0:1], rel_f.rearrange("p c e -> p (c e)"), AX.X, ALU.max)
                nc.vector.tensor_reduce(chk[:, 1:2], dst_i.rearrange("p c e -> p (c e)"), AX.X, ALU.max)
                nc.vector.tensor_reduce(chk[:, 2:3], firsts[:, 0:c], AX.X, ALU.min)
                nc.vector.tensor_copy(chk[0:ROWS, 3:4], firsts[0:ROWS, c:c + 1])
                nc.vector.tensor_reduce(chk[:, 4:5], rel_f[:, 0:c, :].rearrange("p c e -> p (c e)"), AX.X, ALU.min)
                nc.vector.tensor_reduce(chk[:, 5:6], rel_f[:, c, 0:LAST_E], AX.X, ALU.min)
                link(nc.vector.tensor_reduce(chk[0:ROWS - 1, 6:7], rel_f[0:ROWS - 1, c, LAST_E:BE], AX.X, ALU.min))
                nc.vector.tensor_scalar(chk[:, 0:1], chk[:, 0:1], float(WIN), None, ALU.is_ge)
                nc.vector.tensor_scalar(chk[:, 1:2], chk[:, 1:2], float(N), None, ALU.is_ge)
                link(nc.vector.tensor_scalar(chk[:, 2:7], chk[:, 2:7], 0.0, None, ALU.is_lt))
                nc.vector.tensor_reduce(nviol[:], chk[:, 0:7], AX.X, ALU.add).then_inc(s_viol, 1)
                dve.wait_ge(s_nviol, 1)
                nc.vector.tensor_scalar(gen[0:1, :], ps_viol[0:1, :], 0.5, None, ALU.is_ge).then_inc(s_gen, 1)
                dve.wait_ge(s_gen, 1)

            check()
            dve.wait_ge(s_untab, 2)
            dve.wait_ge(s_pool_clear, 1)

            def one_hots(slot, table, chunk):
                dve.wait_ge(s_mm, chunk + 1)
                starts = rel[:, :, :].rearrange("p b r -> p (b r)")[:, bass.ds(table * (BPC * RUN), BPC * RUN)]
                nc.vector.tensor_tensor(onehot[:, slot, :, :], iota_win[:, :].unsqueeze(1).to_broadcast([P, BPC * RUN, WIN]),
                                        starts.unsqueeze(2).to_broadcast([P, BPC * RUN, WIN]), ALU.is_equal).then_inc(s_onehot, 1)

            def add_sum(slot, b, chunk, batch, node):
                if b == 0:
                    dve.wait_ge(s_mm, chunk + (1 + C_MM))
                dve.wait_ge(s_added, batch + C_ADDED)
                at_node = agg[:, :, bass.ds(node, WIN)]
                o = b * 2 * WIN
                nc.vector.tensor_tensor(at_node, ps_sum[:, slot, o:o + 2 * WIN].rearrange("p (a n) -> p a n", a=2), at_node,
                                        ALU.add).then_inc(s_added, 1)

            def ln1(step, n, x_landed, pair):
                if step == 0:
                    dve.wait_ge(s_xload, x_landed)
                    for j in range(2):
                        last = nc.vector.bn_stats(bn[:, j, :], xn[:, j, :])
                    last.then_inc(s_bn, 1)
                    dve.wait_ge(s_bn, n + 1)
                    apart(dve)
                    for j in range(2):
                        last = nc.vector.bn_aggr(mv[:, 0, j, :], bn[:, j, :])
                    last.then_inc(s_mv, 1)
                elif step == 1:
                    dve.wait_ge(s_std, n + 1)
                    nc.vector.reciprocal(rstd[:, 0, 0:2], std[:, 0, 0:2]).then_inc(s_rstd, 1)
                    dve.wait_ge(s_rstd, n + 1)
                    nc.vector.scalar_tensor_tensor(nmr[:, 0, 0:2], mv[:, 0, 0:2, 0], -1.0, rstd[:, 0, 0:2], ALU.mult,
                                                   ALU.mult).then_inc(s_nmr, 1)
                else:
                    dve.wait_ge(s_self, n + 1)
                    dve.wait_ge(s_xb, n + 2)
                    nc.vector.tensor_tensor(x0[:, bass.ds(pair * 2, 2), :],
                                            ps_self[:, 0:2 * D].rearrange("p (j f) -> p j f", j=2), xb[:, :, :],
                                            ALU.add).then_inc(s_x0, 1)

            def load_bases(chunk):
                both = nc.vector.value_load(base_pair[0:1, bass.ds(chunk, 1)], min_val=0, max_val=(NPAD - WIN) * 65537)
                return [(both & 65535).with_bounds(min_val=0, max_val=NPAD - WIN), (both >> 16).with_bounds(min_val=0, max_val=NPAD - WIN)]

            def run_pass(p):
                if not isinstance(p, int):
                    dve.wait_ge(s_pass, 2 * p - 1)
                    apart(dve)
                    nc.vector.tensor_scalar(rel[:, :, :], rel[:, :, :], float(-WIN), None, ALU.add)
                    nc.vector.tensor_scalar(base[:, :], base[:, :], float(WIN), None, ALU.add).then_inc(s_pass, 1)
                    dve.wait_ge(s_pass, 2 * p)
                    apart(dve)
                for c in range(AHEAD):
                    one_hots(c, c, p * CHUNKS + c)

                def turn(it, start=True, finish=True):
                    x_landed = p * XL + (XL if isinstance(it, int) and it == PAIRS - 1 else it * 16 + 16)
                    for c in range(SLOTS):
                        j = it * SLOTS + c
                        nodes = load_bases(j)
                        batch = p * BATCHES + it * BPT + c * BPC
                        add_sum(c, 0, p * CHUNKS + j, batch, nodes[0])
                        if not (isinstance(it, int) and j + AHEAD >= CHUNKS):
                            one_hots((c + AHEAD) % SLOTS, j + AHEAD, p * CHUNKS + j + AHEAD)
                        add_sum(c, 1, p * CHUNKS + j, batch + 1, nodes[1])
                        if start and c == 0:
                            ln1(0, p * PAIRS + it, x_landed, it)
                        if finish and c == 1:
                            ln1(2, p * PAIRS + it - 1, x_landed, it - 1)
                        if start and c == 1:
                            ln1(1, p * PAIRS + it, x_landed, it)

                turns(dve, turn)
                add_sum(0, 0, p * CHUNKS + TURNS * SLOTS, p * BATCHES + TURNS * BPT, load_bases(CHUNKS - 1)[0])
                dve.wait_ge(s_added, p * BATCHES + (BATCHES + C_ADDED))
                if not isinstance(p, int):
                    apart(dve)
                    dve.sem_inc(s_pass, 1)

            def setup():
                nc.vector.memset(agg[:, 0, :], 0.0)
                nc.vector.memset(agg[:, 1, :], 0.0)
                nc.vector.memset(base[:, :], -WIN)
                nc.vector.memset(dst_i[:, ROUNDS - 1, :], -1).then_inc(s_dst_clear, 1)
                dve.wait_ge(s_dst, 96)
                nc.vector.tensor_scalar(rel_f, dst_i, float(WIN), None, ALU.add).then_inc(s_relf, 1)
                dve.wait_ge(s_turn, 3)
                copy_table()
                dve.wait_ge(s_untab, 3)
                dve.sem_inc(s_pass, 1)

            done = all_passes(dve, run_pass, setup)
            dve.wait_ge(s_added, done)

            nc.vector.memset(x0[:, NT:GROUPS * GN, :], 0.0).then_inc(s_deg, 1)
            dve.wait_ge(s_deg, 1)

            def x_after_layer0(g, u):
                dve.wait_ge(s_nb, g + 3)
                nb = ps_nb[u][:, :, 0:2 * (D + 1)].rearrange("p b (t c) -> p b t c", t=2)
                nc.vector.tensor_scalar(deg[:, :].rearrange("p (b t) -> p b t", b=2), nb[:, :, :, D], 1.0, None,
                                        ALU.max).then_inc(s_deg, 1)
                dve.wait_ge(s_deg, 2 * g + 2)
                nc.vector.reciprocal(rdeg[:, :], deg[:, :]).then_inc(s_deg, 1)
                dve.wait_ge(s_deg, 2 * g + 3)
                for j in range(GN):
                    row = x0[:, bass.ds(g * GN + j, 1), :].rearrange("p o f -> p (o f)")
                    last = nc.vector.scalar_tensor_tensor(row, nb[:, j // 2, j % 2, 0:D], rdeg[:, j:j + 1], row,
                                                          ALU.mult, ALU.add)
                last.then_inc(s_x1, 1)
                dve.wait_ge(s_x1, g + 3)
                apart(dve)
                for j in range(GN):
                    last = nc.vector.bn_stats(bn[:, j, :], x0[:, bass.ds(g * GN + j, 1), :].rearrange("p o f -> p (o f)"))
                last.then_inc(s_bn2, 1)
                dve.wait_ge(s_bn2, g + 1)
                apart(dve)
                for j in range(GN):
                    last = nc.vector.bn_aggr(mv[:, u, j, :], bn[:, j, :])
                last.then_inc(s_mv2, 1)

            def scale2(g, u):
                dve.wait_ge(s_std2, g + 1)
                nc.vector.reciprocal(rstd[:, u, :], std[:, u, :]).then_inc(s_rstd2, 1)
                dve.wait_ge(s_rstd2, g + 1)
                nc.vector.scalar_tensor_tensor(nmr[:, u, :], mv[:, u, :, 0], -1.0, rstd[:, u, :], ALU.mult,
                                               ALU.mult).then_inc(s_nmr2, 1)

            def result(g, u, stored):
                dve.wait_ge(s_o, g + 3)
                dve.wait_ge(s_x1b, g + 1)
                dve.wait_ge(s_store[u], stored)
                nc.vector.tensor_tensor(y[:, u, :, :], ps_out[u].rearrange("p (t f) -> p t f", t=GN), x1b[:, u, :, :],
                                        ALU.add).then_inc(s_y, 1)

            for g in range(2):
                x_after_layer0(g, g)
                scale2(g, g)
            with dve.Fori(0, GROUPS // 2 - 1) as it:
                for u in range(2):
                    x_after_layer0(2 * it + (u + 2), u)
                    scale2(2 * it + (u + 2), u)
                    result(2 * it + u, u, 16 * it + 16)
            for g in range(GROUPS - 3, GROUPS):
                if g + 2 < GROUPS:
                    x_after_layer0(g + 2, g % 2)
                    scale2(g + 2, g % 2)
                result(g, g % 2, 16 * (g // 2) + 16)


_USED = ['x', 'dst', 'edge_attr_128', 'edge_attr_64', 'L0_gnn_W_self', 'L0_gnn_W_neigh', 'L0_gnn_W_edge',
         'L0_gnn_W_final', 'L0_gnn_b_final', 'L1_gnn_W1', 'L1_gnn_b1', 'L1_gnn_W2', 'L1_gnn_b2']


def kernel(**inputs):
    import numpy as _np
    import concourse.bacc as _bacc
    from concourse import mybir as _mybir
    from concourse.bass_utils import run_bass_kernel_spmd as _run

    nc = _bacc.Bacc("TRN2", target_bir_lowering=False, num_devices=1)
    arrays, args = {}, []
    for name in _USED:
        a = _np.ascontiguousarray(inputs[name])
        arrays[f"in_{name}_dram"] = a
        args.append(nc.dram_tensor(f"in_{name}_dram", a.shape, _mybir.dt.from_np(a.dtype), kind="ExternalInput").ap())
    args.append(nc.dram_tensor("out_0_dram", inputs['x'].shape, _mybir.dt.float32, kind="ExternalOutput").ap())
    build_gnn(nc, *args)
    r = _run(nc, [arrays], core_ids=[0])
    return r.results[0]["out_0_dram"]
```

```python
from contextlib import ExitStack

import concourse.bass as bass
from concourse import mybir

F32 = mybir.dt.float32
BF16 = mybir.dt.bfloat16
I16 = mybir.dt.int16
I32 = mybir.dt.int32
ALU = mybir.AluOpType
ACT = mybir.ActivationFunctionType
AX = mybir.AxisListType
DVE_ONLY = [mybir.EngineType.DVE]

P = 128
EPS = 1e-5


def build_gnn(nc, x, dst, edge_attr_128, edge_attr_64, W_self, W_neigh, W_edge, W_final, b_final,
              W1, b1, W2, b2, out):
    N, D = x.shape
    E = dst.shape[0]
    D64 = edge_attr_64.shape[1]
    H = P // 2
    assert D == P and D64 == H

    WIN = 64
    RUN = 3
    BE = RUN * P
    BPC = 2
    SLOTS = 5
    AHEAD = 3
    BATCHES = -(-E // BE)
    CHUNKS = -(-BATCHES // BPC)
    TURNS = CHUNKS // SLOTS
    BPT = BPC * SLOTS
    CE = BPC * BE
    LAST_E = E - (BATCHES - 1) * BE
    LAST_R = LAST_E // RUN
    assert CHUNKS == TURNS * SLOTS + 1 and BATCHES % BPC == 1 and LAST_E > LAST_R * RUN
    ROUNDS = -(-BATCHES // P)
    ROWS = BATCHES - (ROUNDS - 1) * P

    NT = -(-N // P)
    GN = 4
    GROUPS = -(-NT // GN)
    GW = GN * P
    NPAD = GROUPS * GW
    LAST_N = N - (NT - 1) * P
    PAIRS = NT // 2
    assert PAIRS * 2 == NT and PAIRS + 1 <= TURNS and GROUPS % 2 == 1 and GROUPS >= 7
    GEN_PASSES = -(-N // WIN)
    assert GEN_PASSES * WIN <= NPAD and N <= NPAD - WIN

    with ExitStack() as ctx:
        def sb(name, shape, dt=F32):
            return ctx.enter_context(nc.sbuf_tensor(name, shape, dt))

        def psum(name, shape):
            return ctx.enter_context(nc.psum_tensor(name, shape, F32))

        def sem(name):
            return ctx.enter_context(nc.semaphore(name))

        agg = sb("agg", [P, 2, NPAD])
        x0 = sb("x0", [P, GROUPS * GN, D])
        ring128 = sb("ring128", [P, SLOTS, BPC, RUN * D])
        ring64 = sb("ring64", [P, SLOTS, BPC, RUN * D64])
        rel = sb("rel", [P, CHUNKS * BPC, RUN])
        base = sb("base", [1, CHUNKS * BPC], I16)
        base_pair = base[0:1, :].bitcast(I32)
        onehot = sb("onehot", [P, SLOTS, BPC * RUN, WIN])
        xn = sb("xn", [P, 2, D])
        xb = sb("xb", [P, 2, D])
        hn = sb("hn", [P, 2, D])
        hT = sb("hT", [P, 2, P])
        w_a = sb("w_a", [P, D])
        w_c = sb("w_c", [P, D + 1])
        w1a = sb("w1a", [P, D])
        w1b = sb("w1b", [P, D])
        w2 = sb("w2", [P, D])
        b0_bc = sb("b0_bc", [P, D])
        b2_bc = sb("b2_bc", [P, D])
        b1_col = sb("b1_col", [P, 1])
        ident = sb("ident", [P, P])
        ones_f = sb("ones_f", [P, P])
        ones_h = sb("ones_h", [P, H], BF16)
        iota_win = sb("iota_win", [P, WIN])
        eps = sb("eps", [P, 1])
        bn = sb("bn", [P, GN, 6])
        mv = sb("mv", [P, 2, GN, 2])
        std = sb("std", [P, 2, GN])
        rstd = sb("rstd", [P, 2, GN])
        nmr = sb("nmr", [P, 2, GN])
        deg = sb("deg", [P, GN])
        rdeg = sb("rdeg", [P, GN])
        chk = sb("chk", [P, 4 * ROUNDS + 1])
        nviol = sb("nviol", [P, 1])
        minus_mean = sb("minus_mean", [P, 2])
        gen = sb("gen", [1, 1], I32)

        flat = x0[:, :, :].rearrange("p t f -> p (t f)")
        at = [0]

        def scratch(cols):
            at[0] += cols
            assert at[0] <= NPAD
            return flat[:, at[0] - cols:at[0]]

        dst_i = scratch(ROUNDS * BE).bitcast(I32).rearrange("p (c e) -> p c e", c=ROUNDS)
        rel_f = scratch(ROUNDS * BE).rearrange("p (c e) -> p c e", c=ROUNDS)
        firsts = scratch(ROUNDS)
        ws_raw, wn_raw, we_raw = scratch(D), scratch(D), scratch(D64)
        wf_raw = scratch(2 * D)
        wfT = scratch(2 * D).rearrange("p (h o) -> p h o", h=2)
        t1 = scratch(D)

        r128 = ring128[:, :, :, :].rearrange("p s b f -> p (s b f)")
        stage64 = r128[:, 0:2 * GW].rearrange("p (b n) -> p b n", b=2)
        h2 = r128[:, 2 * GW:4 * GW].rearrange("p (b t f) -> p b t f", b=2, t=GN)
        x1b = r128[:, 4 * GW:6 * GW].rearrange("p (b t f) -> p b t f", b=2, t=GN)
        h2T = r128[:, 6 * GW:7 * GW]
        r64 = ring64[:, :, :, :].rearrange("p s b f -> p (s b f)")
        y = r64[:, 0:2 * GW].rearrange("p (b t f) -> p b t f", b=2, t=GN)
        hid = r64[:, 2 * GW:3 * GW]

        ps = psum("ps", [P, 8, 512])
        ps_sum = ps[:, 0:SLOTS, :]
        ps_tp, ps_self = ps[:, 5, :], ps[:, 6, :]
        ps_tab = ps[:, 0:4, :].rearrange("p b n -> p (b n)")
        ps_base = ps[0:1, 5:7, :].rearrange("p b n -> p (b n)")
        ps_w, ps_viol = ps[:, 7, :], ps[:, 7, 0:1]
        ps_nb = (ps[:, 0:2, :], ps[:, 2:4, :])
        ps_t2, ps_hid = ps[:, 4, :], ps[:, 7, :]
        ps_out = (ps[:, 5, :], ps[:, 6, :])

        s_const = sem("s_const")
        s_waits_passed = sem("s_waits_passed")
        s_dve = sem("s_dve")
        s_dst_clear = sem("s_dst_clear")
        s_dst = sem("s_dst")
        s_relf = sem("s_relf")
        s_turn = sem("s_turn")
        s_untab = sem("s_untab")
        s_clear = sem("s_clear")
        s_w = sem("s_w")
        s_wps = sem("s_wps")
        s_wsb = sem("s_wsb")
        s_viol = sem("s_viol")
        s_nviol = sem("s_nviol")
        s_gen = sem("s_gen")
        s_load = [sem(f"s_load{i}") for i in range(SLOTS)]
        s_onehot = sem("s_onehot")
        s_mm = sem("s_mm")
        s_added = sem("s_added")
        s_pass = sem("s_pass")
        s_xload = sem("s_xload")
        s_bn, s_mv, s_std, s_rstd, s_minus, s_scaled = (sem(n) for n in ("s_bn", "s_mv", "s_std", "s_rstd", "s_minus", "s_scaled"))
        s_h, s_tp, s_ht, s_self, s_xb, s_x0 = (sem(n) for n in ("s_h", "s_tp", "s_ht", "s_self", "s_xb", "s_x0"))
        s_stage, s_nb, s_deg, s_x1 = (sem(n) for n in ("s_stage", "s_nb", "s_deg", "s_x1"))
        s_bn2, s_mv2, s_std2, s_rstd2, s_nmr2 = (sem(n) for n in ("s_bn2", "s_mv2", "s_std2", "s_rstd2", "s_nmr2"))
        s_h2, s_t2, s_h2t, s_hid, s_hr = (sem(n) for n in ("s_h2", "s_t2", "s_h2t", "s_hid", "s_hr"))
        s_o, s_x1b, s_y = (sem(n) for n in ("s_o", "s_x1b", "s_y"))
        s_y_free = sem("s_y_free")
        s_store = [sem(f"s_store{i}") for i in range(2)]

        C_MM, C_ADDED = SLOTS, BPT
        XL = 16 * (PAIRS + 1)
        N_CONST = 9
        DVE_CLEARS = NPAD * 3 // 8
        WARM_UP = 16
        KEEPERS = 1

        block = ctx.enter_context(nc.Block())

        def general(eng):
            eng.wait_ge(s_gen, 1)
            return eng.value_load(gen[0:1, 0:1], min_val=0, max_val=1)

        def all_passes(eng, run_pass, setup=None, verdict=None):
            run_pass(0)
            if verdict is not None:
                verdict()
            again = general(eng)
            with eng.If(again > 0):
                if setup is not None:
                    setup()
                with eng.Fori(1, GEN_PASSES + 1) as p:
                    run_pass(p)
            return again * (GEN_PASSES * BATCHES) + (BATCHES + C_ADDED)

        def turns(eng, turn):
            turn(0, finish=False)
            with eng.Fori(1, PAIRS - 1) as it:
                turn(it)
            turn(PAIRS - 1)
            turn(PAIRS, start=False)
            for it in range(PAIRS + 1, TURNS):
                turn(it, start=False, finish=False)

        def steps(eng, step, ahead, behind):
            k0 = behind
            turns2 = (GROUPS - ahead - behind) // 2
            for k in range(-ahead, k0):
                step(k, k % 2)
            with eng.Fori(0, turns2) as it:
                for u in range(2):
                    step(2 * it + (k0 + u), (k0 + u) % 2)
            for k in range(k0 + 2 * turns2, GROUPS + behind):
                step(k, k % 2)

        def exists(g):
            return not isinstance(g, int) or 0 <= g < GROUPS

        def landed(p, it, slot):
            return p * (32 * TURNS + (64 if slot == 0 else 0)) + it * 32 + (64 if isinstance(it, int) and it == TURNS else 32)

        def apart(eng):
            eng.sem_inc(s_waits_passed, 1)

        @block.sync
        def _(sp):
            def load_dst(times):
                sp.wait_ge(s_dst_clear, times)
                full = (ROUNDS - 1) * P * BE
                whole = (ROWS - 1) * BE
                sp.dma_start(dst_i[:, 0:ROUNDS - 1, :],
                             dst[0:full].rearrange("(c r e) -> r c e", c=ROUNDS - 1, r=P)).then_inc(s_dst, 16)
                sp.dma_start(dst_i[0:ROWS - 1, ROUNDS - 1, :],
                             dst[full:full + whole].rearrange("(r e) -> r e", e=BE)).then_inc(s_dst, 16)
                sp.dma_start(dst_i[ROWS - 1:ROWS, ROUNDS - 1, 0:LAST_E],
                             dst[E - LAST_E:E].rearrange("(r e) -> r e", r=1)).then_inc(s_dst, 16)

            def run_pass(p):
                if not isinstance(p, int):
                    sp.wait_ge(s_mm, p * CHUNKS + C_MM)
                    apart(sp)

                with sp.Fori(0, TURNS) as it:
                    for c in range(SLOTS):
                        sp.wait_ge(s_mm, p * CHUNKS + it * SLOTS + (c + 1))
                        edges = bass.ds(it * (SLOTS * CE) + c * CE, CE)
                        sp.dma_start(ring128[:, c, :, :], edge_attr_128[edges, :].rearrange(
                            "(b p r) f -> p b (r f)", p=P, r=RUN)).then_inc(s_load[c], 16)
                        sp.dma_start(ring64[:, c, :, :], edge_attr_64[edges, :].rearrange(
                            "(b p r) f -> p b (r f)", p=P, r=RUN)).then_inc(s_load[c], 16)

                sp.wait_ge(s_mm, p * CHUNKS + TURNS * SLOTS + 1)
                e0 = (BATCHES - 1) * BE
                e1 = e0 + LAST_R * RUN
                for ring, feats, w in ((ring128, edge_attr_128, D), (ring64, edge_attr_64, D64)):
                    sp.dma_start(ring[0:LAST_R, 0, 0, :], feats[e0:e1, :].rearrange(
                        "(p r) f -> p (r f)", r=RUN)).then_inc(s_load[0], 16)
                    sp.dma_start(ring[LAST_R:LAST_R + 1, 0, 0, 0:(E - e1) * w], feats[e1:E, :].rearrange(
                        "(p r) f -> p (r f)", p=1)).then_inc(s_load[0], 16)

            load_dst(1)
            all_passes(sp, run_pass, lambda: load_dst(2))

            def store(g, u):
                sp.wait_ge(s_y, g + 3)
                sp.dma_start(out[bass.ds(g * GW, GW), :].rearrange("(j p) f -> p j f", p=P),
                             y[:, u, :, :]).then_inc(s_store[u], 16)

            sp.sem_inc(s_y_free, 2)
            with sp.Fori(0, GROUPS // 2) as it:
                for u in range(2):
                    store(2 * it + u, u)
                for u in range(2):
                    sp.wait_ge(s_store[u], 16 * it + 16)
                    sp.sem_inc(s_y_free, 1)
            g = GROUPS - 1
            sp.wait_ge(s_y, GROUPS + 2)
            for j in range(GN):
                n0 = (g * GN + j) * P
                if n0 < N:
                    n = min(P, N - n0)
                    sp.dma_start(out[n0:n0 + n, :], y[0:n, 0, j, :]).then_inc(s_store[0], 16)
            sp.wait_ge(s_store[0], 16 * (GROUPS // 2 + NT - g * GN))

        @block.gpsimd
        def _(pool):
            own = [0]

            def const(ins):
                own[0] += 1
                ins.then_inc(s_const, 1)
                pool.wait_ge(s_const, own[0])

            const(nc.gpsimd.memset(ident[:], 0.0))
            const(nc.gpsimd.affine_select(out=ident[:], in_=ident[:], compare_op=ALU.not_equal, fill=1.0, base=0,
                                          pattern=[[-1, P]], channel_multiplier=1))
            const(nc.gpsimd.iota(iota_win[:], pattern=[[1, WIN]], base=0, channel_multiplier=0,
                                 allow_small_or_imprecise_dtypes=True))
            const(nc.gpsimd.memset(ones_h[:], 1.0))
            const(nc.gpsimd.memset(ones_f[:], 1.0))
            const(nc.gpsimd.memset(eps[:], EPS))
            const(nc.gpsimd.memset(chk[:], 0.0))
            const(nc.gpsimd.memset(w_c[:], 0.0))
            const(nc.gpsimd.memset(w_c[0:1, D:D + 1], 1.0))
            assert own[0] == N_CONST
            nc.gpsimd.memset(agg[:, 0, DVE_CLEARS:NPAD], 0.0)
            nc.gpsimd.memset(agg[:, 1, :], 0.0).then_inc(s_clear, 1)

            def run_pass(p):
                def turn(it):
                    pool.wait_ge(s_xload, p * XL + (XL if isinstance(it, int) else it * 16 + 16))
                    pool.wait_ge(s_x0, p * PAIRS + it + 1)
                    nc.gpsimd.tensor_tensor(xb[:, :, :], xn[:, :, :],
                                            b0_bc[:, :].unsqueeze(1).to_broadcast([P, 2, D]), ALU.add).then_inc(s_xb, 1)
                    pool.wait_ge(s_xb, p * PAIRS + it + 2)
                    apart(pool)
                    pool.wait_ge(s_scaled, p * PAIRS + it + 2)
                    rows = x0[:, bass.ds(it * 2, 2), :]
                    nc.gpsimd.tensor_tensor(rows, rows, xb[:, :, :], ALU.add).then_inc(s_x0, 1)

                with pool.Fori(0, PAIRS - 1) as it:
                    turn(it)
                turn(PAIRS - 1)

            pool.wait_ge(s_w, 160)
            done = all_passes(pool, run_pass)

            def stage(g, u):
                pool.wait_ge(s_nb, g + 1)
                apart(pool)
                nc.gpsimd.tensor_copy(stage64[:, u, :], agg[:, 1, bass.ds(g * GW, GW)]).then_inc(s_stage, 1)

            def add_b2(g, u):
                pool.wait_ge(s_x1, g + 3)
                pool.wait_ge(s_y, g + 1)
                nc.gpsimd.tensor_tensor(x1b[:, u, :, :], x0[:, bass.ds(g * GN, GN), :],
                                        b2_bc[:, :].unsqueeze(1).to_broadcast([P, GN, D]), ALU.add).then_inc(s_x1b, 1)

            def step(k, u):
                if exists(k):
                    add_b2(k, u)
                if exists(k + 5) and not (isinstance(k, int) and k + 5 < 2):
                    stage(k + 5, 1 - u)

            pool.wait_ge(s_added, done)
            pool.wait_ge(s_stage, 2)
            steps(pool, step, 5, 0)

        @block.tensor
        def _(pe):
            def turn_tables(times):
                pe.wait_ge(s_relf, times)
                for r in range(RUN):
                    for c in range(ROUNDS):
                        k = r * ROUNDS + c
                        last = nc.tensor.transpose(ps_tab[:, k * P:(k + 1) * P],
                                                   rel_f[:, c, :].rearrange("b (p r) -> b r p", r=RUN)[:, r, :], ident[:])
                last.then_inc(s_turn, 1)

            def warm_up():
                for i in range(WARM_UP):
                    nc.tensor.matmul(ps_w[:, 0:P], ones_f[:], ident[:], start=True, stop=True)

            pe.wait_ge(s_const, N_CONST)
            warm_up()
            turn_tables(1)
            for c in range(ROUNDS):
                last = nc.tensor.matmul(ps_base[:, c * P:(c + 1) * P], firsts[:, c:c + 1], ident[:], start=True, stop=True)
            last.then_inc(s_turn, 1)
            pe.sem_inc(s_mm, C_MM)
            pe.wait_ge(s_w, 160)
            for h in range(2):
                last = nc.tensor.transpose(ps_w[:, h * P:(h + 1) * P], wf_raw[:, h * P:(h + 1) * P], ident[:])
            last.then_inc(s_wps, 1)
            pe.wait_ge(s_wsb, 1)
            nc.tensor.matmul(ps_w[:, 0:D], ws_raw, wfT[:, 0, :], start=True, stop=True)
            nc.tensor.matmul(ps_w[:, D:2 * D], wn_raw, wfT[:, 1, :], start=True, stop=True).then_inc(s_wps, 1)
            pe.wait_ge(s_wsb, 2)
            nc.tensor.matmul(ps_w[H:P, 0:D], we_raw, t1, start=True, stop=True).then_inc(s_wps, 1)
            pe.wait_ge(s_untab, 2)
            pe.wait_ge(s_wsb, 3)
            warm_up()

            def sums(slot, batches, chunk, j, load):
                pe.wait_ge(s_load[slot], load)
                pe.wait_ge(s_onehot, chunk + 1)
                pe.wait_ge(s_added, j)
                hots = onehot[:, slot, :, :].rearrange("p (b r) n -> p b r n", r=RUN)
                halves = onehot[:, slot, :, :].bitcast(BF16).rearrange("p (b r) (n h) -> p b r n h", r=RUN, h=2)
                totals = ps_sum[:, slot, 0:BPC * 2 * WIN].rearrange("p (b a n) -> p b a n", b=BPC, a=2)
                for b in range(batches):
                    for r in range(RUN):
                        first, final = r == 0, r == RUN - 1
                        nc.tensor.matmul(totals[0:H, b, 0, :], ring128[:, slot, b, r * D:r * D + H], hots[:, b, r, :],
                                         start=first, stop=final)
                        nc.tensor.matmul(totals[H:P, b, 0, :], ring128[:, slot, b, r * D + H:(r + 1) * D], hots[:, b, r, :],
                                         start=first, stop=final)
                for b in range(batches):
                    for r in range(RUN):
                        nc.tensor.matmul(totals[H:P, b, 1, :], ring64[:, slot, b, r * D64:(r + 1) * D64], hots[:, b, r, :],
                                         start=r == 0, stop=r == RUN - 1)
                for i in range(KEEPERS):
                    nc.tensor.matmul(ps_w[0:H, 0:256], ones_h[:], onehot[:, slot, :, :].bitcast(BF16).rearrange("p t n -> p (t n)")[:, 0:256],
                                     start=True, stop=True)
                for r in range(RUN):
                    last = nc.tensor.matmul(totals[0:H, 0:batches, 1, :], ones_h[:], halves[:, 0:batches, r, :, 1],
                                            start=r == 0, stop=r == RUN - 1)
                last.then_inc(s_mm, 1)

            def self_part(step, n):
                if step == 0:
                    pe.wait_ge(s_h, n + 1)
                    for j in range(2):
                        last = nc.tensor.transpose(ps_tp[:, j * P:(j + 1) * P], hn[:, j, :], ident[:])
                    last.then_inc(s_tp, 1)
                else:
                    pe.wait_ge(s_ht, n + 1)
                    pe.wait_ge(s_scaled, n + 1)
                    for j in range(2):
                        last = nc.tensor.matmul(ps_self[:, j * D:(j + 1) * D], hT[:, j, :], w_a[:], start=True, stop=True)
                    last.then_inc(s_self, 1)

            def run_pass(p):
                def turn(it, start=True, finish=True):
                    if finish:
                        self_part(0, p * PAIRS + it - 1)
                    for c in range(SLOTS):
                        sums(c, BPC, p * CHUNKS + it * SLOTS + c, p * BATCHES + it * BPT + (c + 1) * BPC, landed(p, it, c))
                        if finish and c == 0:
                            self_part(1, p * PAIRS + it - 1)

                turns(pe, turn)
                sums(0, 1, p * CHUNKS + TURNS * SLOTS, p * BATCHES + TURNS * BPT + 1, landed(p, TURNS, 0))
                pe.wait_ge(s_added, p * BATCHES + (BATCHES + C_ADDED))
                apart(pe)

            def setup():
                turn_tables(2)
                pe.wait_ge(s_untab, 3)

            def verdict():
                pe.wait_ge(s_viol, 1)
                nc.tensor.matmul(ps_viol, ones_f[:], nviol[:], start=True, stop=True).then_inc(s_nviol, 1)

            done = all_passes(pe, run_pass, setup, verdict)

            for s in (s_nb, s_o):
                pe.sem_inc(s, 2)
            for s in (s_t2, s_hid):
                pe.sem_inc(s, 1)
            pe.wait_ge(s_added, done)

            def neigh(g, u):
                pe.wait_ge(s_stage, g + 1)
                pe.wait_ge(s_x1, g + 1)
                for j in range(GN):
                    o = (j % 2) * (D + 1)
                    last = nc.tensor.matmul(ps_nb[u][:, j // 2, o:o + D + 1], stage64[:, u, j * P:(j + 1) * P],
                                            w_c[:], start=True, stop=True)
                last.then_inc(s_nb, 1)

            def hidden(g):
                pe.wait_ge(s_hr, g + 1)
                nc.tensor.matmul(ps_hid, w1b[:], agg[:, 0, bass.ds(g * GW, GW)], start=True, stop=False)
                pe.wait_ge(s_h2t, g + 2)
                nc.tensor.matmul(ps_hid, w1a[:], h2T, start=False, stop=True).then_inc(s_hid, 1)

            def turn(g, u):
                pe.wait_ge(s_h2, g + 1)
                pe.wait_ge(s_h2t, g + 1)
                for j in range(GN):
                    last = nc.tensor.transpose(ps_t2[:, j * P:(j + 1) * P], h2[:, u, j, :], ident[:])
                last.then_inc(s_t2, 1)

            def output(g, u):
                pe.wait_ge(s_hr, g + 2)
                pe.wait_ge(s_y, g + 1)
                for j in range(GN):
                    last = nc.tensor.matmul(ps_out[u][:, j * D:(j + 1) * D], hid[:, j * P:(j + 1) * P], w2[:],
                                            start=True, stop=True)
                last.then_inc(s_o, 1)

            def step(k, u):
                if exists(k):
                    hidden(k)
                if exists(k + 1):
                    turn(k + 1, 1 - u)
                if exists(k + 4):
                    neigh(k + 4, u)
                if exists(k):
                    output(k, u)

            steps(pe, step, 4, 0)

        @block.scalar
        def _(act):
            for tile, src in ((ws_raw, W_self), (wn_raw, W_neigh), (wf_raw, W_final), (we_raw, W_edge),
                              (w1a[:], W1[0:D, :]), (w1b[:], W1[D:2 * D, :]), (w2[:], W2),
                              (b0_bc[:], b_final.partition_broadcast(P)), (b2_bc[:], b2.partition_broadcast(P)),
                              (b1_col[:], b1.rearrange("(p o) -> p o", o=1))):
                act.dma_start(tile, src).then_inc(s_w, 16)
            act.wait_ge(s_wps, 1)
            nc.scalar.copy(wfT, ps_w[:, 0:2 * P].rearrange("p (h o) -> p h o", h=2)).then_inc(s_wsb, 1)
            act.wait_ge(s_wps, 2)
            nc.scalar.copy(w_a[:], ps_w[:, 0:D])
            nc.scalar.copy(t1, ps_w[:, D:2 * D]).then_inc(s_wsb, 1)
            act.wait_ge(s_wps, 3)
            act.wait_ge(s_const, N_CONST)
            nc.scalar.copy(w_c[H:P, 0:D], ps_w[H:P, 0:D]).then_inc(s_wsb, 1)

            def load_x(pair):
                if isinstance(pair, int) and pair == PAIRS - 1:
                    n0 = pair * 2 * P
                    act.dma_start(xn[:, 0, :], x[n0:n0 + P, :]).then_inc(s_xload, 16)
                    act.dma_start(xn[0:LAST_N, 1, :], x[n0 + P:N, :]).then_inc(s_xload, 16)
                else:
                    act.dma_start(xn[:, :, :], x[bass.ds(pair * (2 * P), 2 * P), :].rearrange(
                        "(j p) f -> p j f", p=P)).then_inc(s_xload, 16)

            def run_pass(p):
                def turn(it):
                    n = p * PAIRS + it
                    act.wait_ge(s_mv, n + 1)
                    nc.scalar.activation(minus_mean[:, :], mv[:, 0, 0:2, 0], ACT.Copy, scale=-1.0).then_inc(s_minus, 1)
                    nc.scalar.activation(std[:, 0, 0:2], mv[:, 0, 0:2, 1], ACT.Sqrt, bias=eps[:], scale=1.0).then_inc(s_std, 1)
                    act.wait_ge(s_minus, n + 1)
                    apart(act)
                    for j in range(2):
                        last = nc.scalar.activation(hn[:, j, :], xn[:, j, :], ACT.Relu, bias=minus_mean[:, j:j + 1], scale=1.0)
                    last.then_inc(s_h, 1)
                    if not (isinstance(it, int) and it == PAIRS - 1):
                        act.wait_ge(s_h, n + 1)
                        apart(act)
                        act.wait_ge(s_xb, n + 2)
                        apart(act)
                        load_x(it + 1)
                    act.wait_ge(s_tp, n + 1)
                    nc.scalar.copy(hT[:, :, :].rearrange("p j n -> p (j n)"), ps_tp[:, 0:2 * P]).then_inc(s_ht, 1)
                    act.wait_ge(s_rstd, n + 1)
                    apart(act)
                    act.wait_ge(s_self, n + 1)
                    apart(act)
                    for j in range(2):
                        last = nc.scalar.activation(x0[:, bass.ds(it * 2 + j, 1), :].rearrange("p o f -> p (o f)"),
                                                    ps_self[:, j * D:(j + 1) * D], ACT.Identity, scale=rstd[:, 0, j:j + 1])
                    last.then_inc(s_scaled, 1)

                if not isinstance(p, int):
                    act.wait_ge(s_xb, p * PAIRS + 1)
                    apart(act)
                load_x(0)
                with act.Fori(0, PAIRS - 2) as it:
                    turn(it)
                turn(PAIRS - 2)
                turn(PAIRS - 1)

            done = all_passes(act, run_pass)

            for s in (s_h2t, s_hr):
                act.sem_inc(s, 1)
            act.wait_ge(s_added, done)

            def std2(g, u):
                act.wait_ge(s_mv2, g + 1)
                nc.scalar.activation(std[:, u, :], mv[:, u, :, 1], ACT.Sqrt, bias=eps[:], scale=1.0).then_inc(s_std2, 1)

            def norm2(g, u):
                act.wait_ge(s_nmr2, g + 1)
                for j in range(GN):
                    last = nc.scalar.activation(h2[:, u, j, :], x0[:, bass.ds(g * GN + j, 1), :].rearrange("p o f -> p (o f)"),
                                                ACT.Relu, bias=nmr[:, u, j:j + 1], scale=rstd[:, u, j:j + 1])
                last.then_inc(s_h2, 1)

            def hidden(g):
                act.wait_ge(s_hid, g + 2)
                act.wait_ge(s_o, g + 2)
                nc.scalar.activation(hid, ps_hid, ACT.Relu, bias=b1_col[:], scale=1.0).then_inc(s_hr, 1)

            def turn(g):
                act.wait_ge(s_t2, g + 2)
                act.wait_ge(s_hid, g + 1)
                nc.scalar.copy(h2T, ps_t2).then_inc(s_h2t, 1)

            def step(k, u):
                if exists(k):
                    hidden(k)
                if exists(k + 1):
                    turn(k + 1)
                if exists(k + 2):
                    norm2(k + 2, u)
                if exists(k + 3):
                    std2(k + 3, 1 - u)

            steps(act, step, 3, 0)

        @block.vector
        def _(dve):
            own = [0]

            def link(ins):
                own[0] += 1
                ins.then_inc(s_dve, 1)
                dve.wait_ge(s_dve, own[0])

            def copy_table():
                nc.vector.tensor_copy(rel[:, :, :].rearrange("p b r -> p r b"),
                                      ps_tab[:, 0:RUN * ROUNDS * P].rearrange("p (r b) -> p r b", r=RUN)[:, :, 0:CHUNKS * BPC]
                                      ).then_inc(s_untab, 1)

            nc.vector.memset(dst_i[:, ROUNDS - 1, :], -1).then_inc(s_dst_clear, 1)
            nc.vector.memset(agg[:, 0, 0:DVE_CLEARS], 0.0).then_inc(s_clear, 1)
            dve.sem_inc(s_added, C_ADDED)
            for s in (s_x0, s_xb, s_scaled):
                dve.sem_inc(s, 1)
            for s in (s_x1, s_y):
                dve.sem_inc(s, 2)
            dve.wait_ge(s_dst, 48)
            nc.vector.tensor_copy(firsts, dst_i[:, :, 0])
            nc.vector.tensor_tensor(rel_f, dst_i, dst_i[:, :, 0:1].to_broadcast([P, ROUNDS, BE]), ALU.subtract).then_inc(s_relf, 1)
            dve.wait_ge(s_turn, 1)
            copy_table()
            dve.wait_ge(s_turn, 2)
            nc.vector.tensor_scalar(base[0:1, :], ps_base[:, 0:CHUNKS * BPC], 0.0, float(NPAD - WIN), ALU.max,
                                    ALU.min).then_inc(s_untab, 1)

            def check():
                R, c = ROUNDS, ROUNDS - 1
                most, highest, least, lowest = (chk[:, i * R:(i + 1) * R] for i in range(4))
                link(nc.vector.tensor_reduce(most, rel_f, AX.X, ALU.max))
                nc.vector.tensor_tensor(highest, most, firsts, ALU.add)
                nc.vector.tensor_reduce(least[:, 0:c], rel_f[:, 0:c, :], AX.X, ALU.min)
                nc.vector.tensor_reduce(least[:, c:c + 1], rel_f[:, c, 0:LAST_E], AX.X, ALU.min)
                nc.vector.tensor_reduce(chk[0:ROWS - 1, 4 * R:4 * R + 1], rel_f[0:ROWS - 1, c, LAST_E:BE], AX.X, ALU.min)
                nc.vector.tensor_copy(lowest[:, 0:c], firsts[:, 0:c])
                link(nc.vector.tensor_copy(lowest[0:ROWS, c:c + 1], firsts[0:ROWS, c:c + 1]))
                nc.vector.tensor_scalar(most, most, float(WIN), None, ALU.is_ge)
                nc.vector.tensor_scalar(highest, highest, float(N), None, ALU.is_ge)
                link(nc.vector.tensor_scalar(chk[:, 2 * R:4 * R + 1], chk[:, 2 * R:4 * R + 1], 0.0, None, ALU.is_lt))
                nc.vector.tensor_reduce(nviol[:], chk[:, :], AX.X, ALU.add).then_inc(s_viol, 1)

            def verdict():
                dve.wait_ge(s_nviol, 1)
                nc.vector.tensor_scalar(gen[0:1, :], ps_viol[0:1, :], 0.5, None, ALU.is_ge).then_inc(s_gen, 1)

            dve.wait_ge(s_untab, 2)
            dve.wait_ge(s_const, N_CONST)

            def one_hots(slot, table):
                starts = rel[:, :, :].rearrange("p b r -> p (b r)")[:, bass.ds(table * (BPC * RUN), BPC * RUN)]
                nc.vector.tensor_tensor(onehot[:, slot, :, :], iota_win[:, :].unsqueeze(1).to_broadcast([P, BPC * RUN, WIN]),
                                        starts.unsqueeze(2).to_broadcast([P, BPC * RUN, WIN]), ALU.is_equal).then_inc(s_onehot, 1)

            def add_sum(slot, b, chunk, batch, node):
                if b == 0:
                    dve.wait_ge(s_mm, chunk + (1 + C_MM))
                dve.wait_ge(s_added, batch + C_ADDED)
                at_node = agg[:, :, bass.ds(node, WIN)]
                o = b * 2 * WIN
                nc.vector.tensor_tensor(at_node, ps_sum[:, slot, o:o + 2 * WIN].rearrange("p (a n) -> p a n", a=2), at_node,
                                        ALU.add).then_inc(s_added, 1)

            def ln1(step, n, x_landed):
                if step == 0:
                    dve.wait_ge(s_xload, x_landed)
                    for j in range(2):
                        last = nc.vector.bn_stats(bn[:, j, :], xn[:, j, :])
                    last.then_inc(s_bn, 1)
                elif step == 1:
                    dve.wait_ge(s_bn, n + 1)
                    apart(dve)
                    for j in range(2):
                        last = nc.vector.bn_aggr(mv[:, 0, j, :], bn[:, j, :])
                    last.then_inc(s_mv, 1)
                else:
                    dve.wait_ge(s_std, n + 1)
                    nc.vector.reciprocal(rstd[:, 0, 0:2], std[:, 0, 0:2]).then_inc(s_rstd, 1)

            def load_bases(chunk):
                _, (both,) = nc.values_load_multi_w_load_instructions(
                    base_pair[0:1, bass.ds(chunk, 1)], engines=DVE_ONLY, min_val=0, max_val=(NPAD - WIN) * 65537,
                    skip_runtime_bounds_check_because="the table is clamped when it is made")
                return [(both & 65535).with_bounds(min_val=0, max_val=NPAD - WIN), (both >> 16).with_bounds(min_val=0, max_val=NPAD - WIN)]

            def run_pass(p):
                if not isinstance(p, int):
                    dve.wait_ge(s_pass, 2 * p - 1)
                    apart(dve)
                    nc.vector.tensor_scalar(rel[:, :, :], rel[:, :, :], float(-WIN), None, ALU.add)
                    nc.vector.tensor_scalar(base[:, :], base[:, :], float(WIN), None, ALU.add).then_inc(s_pass, 1)
                    dve.wait_ge(s_pass, 2 * p)
                    apart(dve)
                for c in range(AHEAD):
                    one_hots(c, c)
                if isinstance(p, int):
                    check()
                    dve.wait_ge(s_clear, 2)

                def turn(it, start=True, finish=True):
                    x_landed = p * XL + (XL if isinstance(it, int) and it == PAIRS - 1 else it * 16 + 16)
                    for c in range(SLOTS):
                        j = it * SLOTS + c
                        nodes = load_bases(j)
                        batch = p * BATCHES + it * BPT + c * BPC
                        add_sum(c, 0, p * CHUNKS + j, batch, nodes[0])
                        if start and 0 < c < 3:
                            ln1(c, p * PAIRS + it, x_landed)
                        if not (isinstance(it, int) and j + AHEAD >= CHUNKS):
                            one_hots((c + AHEAD) % SLOTS, j + AHEAD)
                        add_sum(c, 1, p * CHUNKS + j, batch + 1, nodes[1])
                        if start and c == 0:
                            ln1(c, p * PAIRS + it, x_landed)

                turns(dve, turn)
                add_sum(0, 0, p * CHUNKS + TURNS * SLOTS, p * BATCHES + TURNS * BPT, load_bases(CHUNKS - 1)[0])
                dve.wait_ge(s_x0, p * PAIRS + (PAIRS + 1))
                apart(dve)
                dve.wait_ge(s_added, p * BATCHES + (BATCHES + C_ADDED))
                if not isinstance(p, int):
                    apart(dve)
                    dve.sem_inc(s_pass, 1)

            def setup():
                nc.vector.memset(agg[:, 0, :], 0.0)
                nc.vector.memset(agg[:, 1, :], 0.0)
                nc.vector.memset(base[:, :], -WIN)
                nc.vector.memset(dst_i[:, ROUNDS - 1, :], -1).then_inc(s_dst_clear, 1)
                dve.wait_ge(s_dst, 96)
                nc.vector.tensor_scalar(rel_f, dst_i, float(WIN), None, ALU.add).then_inc(s_relf, 1)
                dve.wait_ge(s_turn, 3)
                copy_table()
                dve.wait_ge(s_untab, 3)
                dve.sem_inc(s_pass, 1)

            done = all_passes(dve, run_pass, setup, verdict)
            dve.wait_ge(s_added, done)

            nc.vector.memset(x0[:, NT:GROUPS * GN, :], 0.0).then_inc(s_deg, 1)
            dve.wait_ge(s_deg, 1)
            for g in range(2):
                nc.vector.tensor_copy(stage64[:, g, :], agg[:, 1, g * GW:(g + 1) * GW]).then_inc(s_stage, 1)

            def degree(g, u):
                dve.wait_ge(s_nb, g + 3)
                nb = ps_nb[u][:, :, 0:2 * (D + 1)].rearrange("p b (t c) -> p b t c", t=2)
                nc.vector.tensor_scalar(deg[:, :].rearrange("p (b t) -> p b t", b=2), nb[:, :, :, D], 1.0, None,
                                        ALU.max).then_inc(s_deg, 1)
                return nb

            def reciprocals(g):
                dve.wait_ge(s_deg, 2 * g + 2)
                nc.vector.reciprocal(rdeg[:, :], deg[:, :]).then_inc(s_deg, 1)

            def x_after_layer0(g, nb):
                dve.wait_ge(s_deg, 2 * g + 3)
                for j in range(GN):
                    row = x0[:, bass.ds(g * GN + j, 1), :].rearrange("p o f -> p (o f)")
                    last = nc.vector.scalar_tensor_tensor(row, nb[:, j // 2, j % 2, 0:D], rdeg[:, j:j + 1], row,
                                                          ALU.mult, ALU.add)
                last.then_inc(s_x1, 1)

            def statistics(g, u):
                dve.wait_ge(s_x1, g + 3)
                apart(dve)
                for j in range(GN):
                    last = nc.vector.bn_stats(bn[:, j, :], x0[:, bass.ds(g * GN + j, 1), :].rearrange("p o f -> p (o f)"))
                last.then_inc(s_bn2, 1)
                dve.wait_ge(s_bn2, g + 1)
                apart(dve)
                for j in range(GN):
                    last = nc.vector.bn_aggr(mv[:, u, j, :], bn[:, j, :])
                last.then_inc(s_mv2, 1)

            def scale2(g, u):
                dve.wait_ge(s_std2, g + 1)
                nc.vector.reciprocal(rstd[:, u, :], std[:, u, :]).then_inc(s_rstd2, 1)

            def shift2(g, u):
                dve.wait_ge(s_rstd2, g + 1)
                nc.vector.scalar_tensor_tensor(nmr[:, u, :], mv[:, u, :, 0], -1.0, rstd[:, u, :], ALU.mult,
                                               ALU.mult).then_inc(s_nmr2, 1)

            def result(g, u):
                dve.wait_ge(s_o, g + 3)
                dve.wait_ge(s_x1b, g + 1)
                dve.wait_ge(s_y_free, g + 1)
                nc.vector.tensor_tensor(y[:, u, :, :], ps_out[u].rearrange("p (t f) -> p t f", t=GN), x1b[:, u, :, :],
                                        ALU.add).then_inc(s_y, 1)

            def step(k, u):
                if exists(k + 3):
                    nb = degree(k + 3, 1 - u)
                if exists(k - 1):
                    result(k - 1, 1 - u)
                if exists(k + 3):
                    reciprocals(k + 3)
                if exists(k + 2):
                    scale2(k + 2, u)
                if exists(k + 3):
                    x_after_layer0(k + 3, nb)
                if exists(k + 2):
                    shift2(k + 2, u)
                if exists(k + 3):
                    statistics(k + 3, 1 - u)

            steps(dve, step, 3, 1)


_USED = ['x', 'dst', 'edge_attr_128', 'edge_attr_64', 'L0_gnn_W_self', 'L0_gnn_W_neigh', 'L0_gnn_W_edge',
         'L0_gnn_W_final', 'L0_gnn_b_final', 'L1_gnn_W1', 'L1_gnn_b1', 'L1_gnn_W2', 'L1_gnn_b2']


def kernel(**inputs):
    import numpy as _np
    import concourse.bacc as _bacc
    from concourse import mybir as _mybir
    from concourse.bass_utils import run_bass_kernel_spmd as _run

    nc = _bacc.Bacc("TRN2", target_bir_lowering=False, num_devices=1)
    arrays, args = {}, []
    for name in _USED:
        a = _np.ascontiguousarray(inputs[name])
        arrays[f"in_{name}_dram"] = a
        args.append(nc.dram_tensor(f"in_{name}_dram", a.shape, _mybir.dt.from_np(a.dtype), kind="ExternalInput").ap())
    args.append(nc.dram_tensor("out_0_dram", inputs['x'].shape, _mybir.dt.float32, kind="ExternalOutput").ap())
    build_gnn(nc, *args)
    r = _run(nc, [arrays], core_ids=[0])
    return r.results[0]["out_0_dram"]
```
